# Optimizing a Trainium2 kernel written in Bass

```python
import numpy as np
import jax
import jax.numpy as jnp

def _softmax(x, axis=-1):
    return jax.nn.softmax(x, axis=axis)

def _gelu(x):
    return jax.nn.gelu(x, approximate=True)

def _silu(x):
    return jax.nn.silu(x)

def _sigmoid(x):
    return jax.nn.sigmoid(x)

def _layernorm(x, axis=-1, eps=1e-05):
    m = jnp.mean(x, axis=axis, keepdims=True)
    v = jnp.var(x, axis=axis, keepdims=True)
    return (x - m) / jnp.sqrt(v + eps)

def _scatter_add(tgt, idx, src, axis=0):
    return tgt.at[idx].add(src)

def _segment_sum(src, seg, n):
    return jax.ops.segment_sum(src, seg, n)
kernel_name = 'mk_cond_resid_d2_seqx_r4_6b83bc'

def setup_inputs(seed: int=0):
    np.random.seed(seed)
    _w = jnp.asarray

    def _rec_inputs():
        import jax
        import jax.numpy as jnp
        _rk = jax.random.key(seed)
        x = -0.000125 + 0.9999 * jax.random.normal(jax.random.fold_in(_rk, 1), (16, 256, 256), jnp.float32)
        _lenS = 256 - jax.random.randint(jax.random.fold_in(_rk, 7), (16,), 0, max(1, 256 // 4) + 1, jnp.int32)
        _lenS2 = 256 - jax.random.randint(jax.random.fold_in(_rk, 8), (16,), 0, max(1, 256 // 4) + 1, jnp.int32)
        cond_8 = jax.random.uniform(jax.random.fold_in(_rk, 11), (16, 8), jnp.float32, 0.0, 0.983423)
        return (x, cond_8)
    x, cond_8 = _rec_inputs()

    def _L0_cond_setup():
        import jax, jax.numpy as jnp
        import numpy as np
        B, S, D = (16, 512, 256)
        E, H = (8, 512)
        key = jax.random.key(seed)
        ks = jax.random.split(key, 8)
        scale = 0.02
        x = jax.random.normal(ks[0], (B, S, D), dtype=jnp.float32)
        opcode_onehot = jax.random.uniform(ks[1], (B, E), dtype=jnp.float32)
        W_up = jax.random.normal(ks[2], (E, H, D), dtype=jnp.float32) * scale
        b_up = jnp.zeros((E, H), dtype=jnp.float32)
        W_gate = jax.random.normal(ks[3], (E, H, D), dtype=jnp.float32) * scale
        b_gate = jnp.zeros((E, H), dtype=jnp.float32)
        W_down = jax.random.normal(ks[4], (E, D, H), dtype=jnp.float32) * scale
        b_down = jnp.zeros((E, D), dtype=jnp.float32)
        return {'x': x, 'opcode_onehot': opcode_onehot, 'W_up': W_up, 'b_up': b_up, 'W_gate': W_gate, 'b_gate': b_gate, 'W_down': W_down, 'b_down': b_down}
    _L0_cond_all = _L0_cond_setup()
    _L0_cond_in = {k: v for k, v in _L0_cond_all.items() if k in ('W_up', 'b_up', 'W_gate', 'b_gate', 'W_down', 'b_down')}
    del _L0_cond_all

    def _L1_cond_setup():
        import jax, jax.numpy as jnp
        import numpy as np
        TOP_K = 2
        NUM_MOE_LAYERS = 12

        def _gemma_mlp(x, gate_w, up_w, down_w):
            g = jnp.einsum('bsh,hi->bsi', x, gate_w)
            u = jnp.einsum('bsh,hi->bsi', x, up_w)
            return jnp.einsum('bsi,ih->bsh', jax.nn.gelu(g, approximate=True) * u, down_w)
        key = jax.random.key(seed)
        ks = jax.random.split(key, 8)
        B, S, H, I, E = (32, 64, 256, 1024, 8)
        std = 0.02
        return {'x': jax.random.normal(ks[0], (B, S, H), jnp.float32), 'router_logits': jax.random.normal(ks[1], (B, E), jnp.float32), 'skill_gate': jax.random.normal(ks[2], (E, H, I), jnp.float32) * std, 'skill_up': jax.random.normal(ks[3], (E, H, I), jnp.float32) * std, 'skill_down': jax.random.normal(ks[4], (E, I, H), jnp.float32) * std, 'shared_gate': jax.random.normal(ks[5], (H, I), jnp.float32) * std, 'shared_up': jax.random.normal(ks[6], (H, I), jnp.float32) * std, 'shared_down': jax.random.normal(ks[7], (I, H), jnp.float32) * std}
    _L1_cond_all = _L1_cond_setup()
    _L1_cond_in = {k: v for k, v in _L1_cond_all.items() if k in ('skill_gate', 'skill_up', 'skill_down', 'shared_gate', 'shared_up', 'shared_down')}
    del _L1_cond_all
    return {'x': x, 'cond_8': cond_8, 'L0_cond_W_up': _L0_cond_in['W_up'], 'L0_cond_b_up': _L0_cond_in['b_up'], 'L0_cond_W_gate': _L0_cond_in['W_gate'], 'L0_cond_b_gate': _L0_cond_in['b_gate'], 'L0_cond_W_down': _L0_cond_in['W_down'], 'L0_cond_b_down': _L0_cond_in['b_down'], 'L1_cond_skill_gate': _L1_cond_in['skill_gate'], 'L1_cond_skill_up': _L1_cond_in['skill_up'], 'L1_cond_skill_down': _L1_cond_in['skill_down'], 'L1_cond_shared_gate': _L1_cond_in['shared_gate'], 'L1_cond_shared_up': _L1_cond_in['shared_up'], 'L1_cond_shared_down': _L1_cond_in['shared_down']}

def reference(x, cond_8, L0_cond_W_up, L0_cond_b_up, L0_cond_W_gate, L0_cond_b_gate, L0_cond_W_down, L0_cond_b_down, L1_cond_skill_gate, L1_cond_skill_up, L1_cond_skill_down, L1_cond_shared_gate, L1_cond_shared_up, L1_cond_shared_down):
    import jax
    import jax.numpy as jnp

    def _L0_cond_ref(x, opcode_onehot, W_up, b_up, W_gate, b_gate, W_down, b_down):
        import jax, jax.numpy as jnp
        import numpy as np
        B, S, D = (16, 512, 256)
        E, H = (8, 512)
        expert = jnp.argmax(opcode_onehot, axis=-1)
        wu, bu = (W_up[expert], b_up[expert])
        wg, bg = (W_gate[expert], b_gate[expert])
        wd, bd = (W_down[expert], b_down[expert])
        up = jnp.einsum('bsd,bhd->bsh', x, wu) + bu[:, None, :]
        gate = jnp.einsum('bsd,bhd->bsh', x, wg) + bg[:, None, :]
        hidden = jax.nn.silu(up) * gate
        out = jnp.einsum('bsh,bdh->bsd', hidden, wd) + bd[:, None, :]
        return out

    def _L1_cond_ref(x, router_logits, skill_gate, skill_up, skill_down, shared_gate, shared_up, shared_down):
        import jax, jax.numpy as jnp
        import numpy as np
        TOP_K = 2
        NUM_MOE_LAYERS = 12

        def _gemma_mlp(x, gate_w, up_w, down_w):
            g = jnp.einsum('bsh,hi->bsi', x, gate_w)
            u = jnp.einsum('bsh,hi->bsi', x, up_w)
            return jnp.einsum('bsi,ih->bsh', jax.nn.gelu(g, approximate=True) * u, down_w)
        B = x.shape[0]
        E = skill_gate.shape[0]
        rw = jax.nn.softmax(router_logits.astype(jnp.float32), axis=-1)
        w, sel = jax.lax.top_k(rw, TOP_K)
        w = w / w.sum(axis=-1, keepdims=True)
        w = w.astype(x.dtype)
        scale = 1.0 / NUM_MOE_LAYERS
        w = scale * w + (1.0 - scale) * jax.lax.stop_gradient(w)
        dense_w = jnp.zeros((B, E), x.dtype).at[jnp.arange(B)[:, None], sel].add(w)

        def step(acc, params):
            g, u, d, we = params
            return (acc + we[:, None, None] * _gemma_mlp(x, g, u, d), None)
        out, _ = jax.lax.scan(step, jnp.zeros_like(x), (skill_gate, skill_up, skill_down, dense_w.T))
        out = out + _gemma_mlp(x, shared_gate, shared_up, shared_down)
        return out
    x = x + _L0_cond_ref(x, cond_8, L0_cond_W_up, L0_cond_b_up, L0_cond_W_gate, L0_cond_b_gate, L0_cond_W_down, L0_cond_b_down)
    x = x + _L1_cond_ref(x, cond_8, L1_cond_skill_gate, L1_cond_skill_up, L1_cond_skill_down, L1_cond_shared_gate, L1_cond_shared_up, L1_cond_shared_down)
    return x

_drawn_inputs = setup_inputs


def setup_inputs(seed=0):
    import zlib

    import numpy as np

    out = dict(_drawn_inputs(seed))
    spreads = {'L0_cond_b_up': (0.0, 0.8), 'L0_cond_b_gate': (0.0, 0.8), 'L0_cond_b_down': (0.0, 0.1)}
    factors = {}
    for name, (base, spread) in spreads.items():
        noise = np.random.default_rng([zlib.crc32(name.encode()), seed]).standard_normal(out[name].shape)
        drawn = base * np.exp(spread * noise) if base else spread * noise
        out[name] = jnp.asarray(drawn.astype(out[name].dtype))
    for name, factor in factors.items():
        out[name] = (out[name] * factor).astype(out[name].dtype)
    return out
```

```python
from contextlib import ExitStack

import concourse.bass as bass
from concourse import mybir

P = 128
ALU = mybir.AluOpType
ACT = mybir.ActivationFunctionType
F32 = mybir.dt.float32
F32R = mybir.dt.float32r
I32 = mybir.dt.int32
U32 = mybir.dt.uint32

NUM_MOE_LAYERS = 12
MIX = 1.0 / NUM_MOE_LAYERS

PLAN = [("S", 0), ("S", 1), ("A", 0), ("A", 1), ("S", 2), ("A", 2), ("A", 3),
        ("L", 0), ("L", 1), ("B", 0), ("B", 1), ("S", 3), ("B", 2), ("B", 3)]
LAST_PLAN = [step for step in PLAN if step[0] != "L"]
NPOS = len(PLAN)
LAG = 2

GATE, UP, DOWN = range(3)
PIECES = 12
SPLIT_AT = {0: [2], 1: [3], 2: [4], 3: [5], 5: [6], 6: [7], 7: [8], 8: [9], 9: [10], 10: [11],
            12: [12], 13: [13]}
LAST_SPLIT_AT = {0: [2], 1: [3], 2: [4], 3: [5], 4: [6], 5: [7], 6: [8], 7: [9], 8: [10], 9: [11]}
SHARED_PIECES = 6
EARLY_PIECES = 2

X_BATCH, UP_BATCH, GATE_BATCH, DOWN_BATCH = 0, 1, 3, 5
BATCHES = 7


def bass_cond_two_layer_kernel(
    nc: bass.Bass,
    x: bass.AP,
    cond: bass.AP,
    up0_w: bass.AP,
    up0_b: bass.AP,
    gate0_w: bass.AP,
    gate0_b: bass.AP,
    down0_w: bass.AP,
    down0_b: bass.AP,
    skill_gate: bass.AP,
    skill_up: bass.AP,
    skill_down: bass.AP,
    shared_gate: bass.AP,
    shared_up: bass.AP,
    shared_down: bass.AP,
    out: bass.AP,
):
    B, S, D = x.shape
    E, H = up0_b.shape
    I = shared_gate.shape[1]
    SC, DC, HC = S // P, D // P, H // P
    HALF = I // 2
    IC = HALF // P
    assert (SC, DC, HC, IC) == (2, 2, 4, 4) and cond.shape == (B, E) and E == 8

    def position(b, j):
        return 2 + NPOS * b + j

    def piece(b, m):
        return SHARED_PIECES + PIECES * b + m

    def batch(s, i):
        return BATCHES * s + i

    ctx = ExitStack()
    with ctx:
        def sb(name, shape, dt=F32):
            return ctx.enter_context(nc.sbuf_tensor(name, shape, dt))

        def bank(name, shape):
            return ctx.enter_context(nc.psum_tensor(name, shape, F32))

        def sem(name):
            return ctx.enter_context(nc.semaphore(name))

        ident = sb("ident", [P, P])
        ident_r = sb("ident_r", [P, P], F32R)
        ones = sb("ones", [B, P])
        logits = sb("logits", [B, E])
        top = sb("top", [B, 8])
        top_at = sb("top_at", [B, 8], U32)
        neg_max = sb("neg_max", [B, 1])
        exps = sb("exps", [B, 8])
        exp_sum = sb("exp_sum", [B, 1])
        exp_inv = sb("exp_inv", [B, 1])
        probs = sb("probs", [B, 2])
        pair_sum = sb("pair_sum", [B, 1])
        pair_inv = sb("pair_inv", [B, 1])
        pair_w = sb("pair_w", [B, 2])
        pair_w2 = sb("pair_w2", [B, 2])
        choice = sb("choice", [B, 4])
        choice_diag = sb("choice_diag", [B, B, 4])
        route = sb("route", [P, B, 4])
        expert = sb("expert", [P, B, 2], I32)
        bias_rows = sb("bias_rows", [E * HC, 2, P])
        bias_down_rows = sb("bias_down_rows", [E * DC, P])
        bias_up = sb("bias_up", [P, E * HC])
        bias_gate = sb("bias_gate", [P, E * HC])
        bias_down = sb("bias_down", [P, E * DC])

        x_raw = sb("x_raw", [P, SC, D])
        up0_raw = sb("up0_raw", [P, HC, D])
        gate0_raw = sb("gate0_raw", [P, HC, D])
        down0_raw = sb("down0_raw", [P, DC, H])
        xT = sb("xT", [P, DC, S])
        xT_hi, xT_lo = sb("xT_hi", [P, DC, S], F32R), sb("xT_lo", [P, DC, S], F32R)
        up0_hi, up0_lo = sb("up0_hi", [P, DC, H], F32R), sb("up0_lo", [P, DC, H], F32R)
        gate0_hi, gate0_lo = sb("gate0_hi", [P, DC, H], F32R), sb("gate0_lo", [P, DC, H], F32R)
        down0_hi, down0_lo = sb("down0_hi", [P, HC, D], F32R), sb("down0_lo", [P, HC, D], F32R)

        x1T = sb("x1T", [P, DC, S])
        x1_hi, x1_lo = sb("x1_hi", [P, DC, S], F32R), sb("x1_lo", [P, DC, S], F32R)
        raw = [[sb(f"raw{r}_{k}", [P, DC * HALF]) for k in ("gate", "up", "down")] for r in range(2)]
        w_hi = [[sb(f"w_hi{r}_{k}", [P, DC * HALF], F32R) for k in ("gate", "up", "down")] for r in range(4)]
        w_lo = [[sb(f"w_lo{r}_{k}", [P, DC * HALF], F32R) for k in ("gate", "up", "down")] for r in range(4)]

        act_out = sb("act_out", [P, 2, 2, S])
        hidden = sb("hidden", [P, 2, 2, S])
        h_hi = [sb(f"h_hi{r}", [P, 2, S], F32R) for r in range(2)]
        h_lo = [sb(f"h_lo{r}", [P, 2, S], F32R) for r in range(2)]
        y = sb("y", [P, SC, D])

        gate_ps = [bank(f"gate_ps{r}", [P, 2, S]) for r in range(2)]
        up_ps = [bank(f"up_ps{r}", [P, 2, S]) for r in range(2)]
        tr_ps = [bank(f"tr_ps{r}", [P, 4, P]) for r in range(2)]
        out_ps = [bank(f"out_ps{r}", [P, 512]) for r in range(2)]

        s_ident0 = sem("ident_zeroed")
        s_ident = sem("ident_ready")
        s_cond = sem("cond_loaded")
        s_bias = sem("bias_loaded")
        s_chain = sem("vector_chain")
        s_top = sem("top_ready")
        s_exp = sem("exps_ready")
        s_diag = sem("choice_diag_ready")
        s_spread = sem("routing_spread")
        s_biasT = sem("bias_transposed")
        s_identr = sem("ident_r_ready")
        s_x = sem("x_loaded")
        s_w0 = [sem(f"layer0_{k}_loaded") for k in ("gate", "up", "down")]
        s_raw = [[sem(f"raw{r}_{k}_loaded") for k in ("gate", "up", "down")] for r in range(2)]
        s_tr = sem("batch_transposed")
        s_tr_hi = sem("batch_hi_ready")
        s_tr_lo = sem("batch_lo_ready")
        s_w_hi = sem("piece_hi_ready")
        s_w_lo = sem("piece_lo_ready")
        s_gu = sem("gate_up_done")
        s_act = sem("act_done")
        s_mul = sem("hidden_done")
        s_h_hi = sem("hidden_hi_ready")
        s_h_lo = sem("hidden_lo_ready")
        s_down = sem("down_done")
        s_x1T = sem("x1T_ready")
        s_x1_hi = sem("x1_hi_ready")
        s_x1_lo = sem("x1_lo_ready")
        s_free = [sem(f"out_bank{r}_read") for r in range(2)]
        s_out = sem("out_stored")

        def half_of(kind, k):
            return k // 2 + (2 if kind == "S" else 0)

        def chunk(r, kind, dc, ic):
            c = dc * HALF + ic * P
            return w_hi[r][kind][:, c:c + P], w_lo[r][kind][:, c:c + P]

        block = ctx.enter_context(nc.Block())

        @block.sync
        def _(sp):
            x_rows = x.rearrange("b (p c) d -> b p c d", c=SC)
            out_rows = out.rearrange("b (p c) d -> b p c d", c=SC)
            layer0_rows = [gate0_w.rearrange("e (c p) d -> e p c d", p=P),
                           up0_w.rearrange("e (c p) d -> e p c d", p=P),
                           down0_w.rearrange("e (c p) h -> e p c h", p=P)]
            layer0_raw = [gate0_raw, up0_raw, down0_raw]
            skill_rows = [skill_gate.rearrange("e (c p) i -> e p c i", p=P),
                          skill_up.rearrange("e (c p) i -> e p c i", p=P),
                          skill_down.rearrange("e (c p) d -> e p c d", p=P)]
            shared_rows = [shared_gate.rearrange("(c p) i -> p c i", p=P),
                           shared_up.rearrange("(c p) i -> p c i", p=P),
                           shared_down.rearrange("(c p) d -> p c d", p=P)]

            def raw_view(r, kind):
                return raw[r][kind][:, :].rearrange("p (c n) -> p c n", c=(IC if kind == DOWN else DC))

            def load_x(s):
                sp.dma_start(x_raw[:, :, :], x_rows[bass.ds(s, 1)].rearrange("o p c d -> (o p) c d")).then_inc(s_x, 16)

            def load_layer0(kind, e):
                sp.dma_start(layer0_raw[kind][:, :, :],
                             layer0_rows[kind][bass.ds(e, 1)].rearrange("o p c d -> (o p) c d")).then_inc(s_w0[kind], 16)

            def load_piece(m, e):
                h, kind = m // 3, m % 3
                k = h % 2
                rows = skill_rows[kind][bass.ds(e, 1)].rearrange("o p c n -> (o p) c n")
                part = rows[:, k * IC:(k + 1) * IC, :] if kind == DOWN else rows[:, :, k * HALF:(k + 1) * HALF]
                sp.dma_start(raw_view(h % 2, kind), part).then_inc(s_raw[h % 2][kind], 16)

            def pick(s, choice_no):
                return sp.value_load(expert[0:1, bass.ds(s, 1), choice_no:choice_no + 1].rearrange("p a b -> p (a b)"),
                                     min_val=0, max_val=E - 1)

            sp.dma_start(logits[:, :], cond[:, :]).then_inc(s_cond, 16)
            load_x(0)
            sp.dma_start(bias_rows[:, 0, :], up0_b.rearrange("e (c p) -> (e c) p", p=P)).then_inc(s_bias, 16)
            sp.dma_start(bias_rows[:, 1, :], gate0_b.rearrange("e (c p) -> (e c) p", p=P)).then_inc(s_bias, 16)
            sp.dma_start(bias_down_rows[:, :], down0_b.rearrange("e (c p) -> (e c) p", p=P)).then_inc(s_bias, 16)
            for kind in (GATE, UP):
                sp.dma_start(raw_view(0, kind), shared_rows[kind][:, :, 0:HALF]).then_inc(s_raw[0][kind], 16)
            sp.wait_ge(s_free[0], 1)
            e_a = pick(0, 0)
            e_b = pick(0, 1)
            for kind in (UP, GATE, DOWN):
                load_layer0(kind, e_a)
            sp.dma_start(raw_view(0, DOWN), shared_rows[DOWN][:, 0:IC, :]).then_inc(s_raw[0][DOWN], 16)
            for kind in (GATE, UP):
                sp.dma_start(raw_view(1, kind), shared_rows[kind][:, :, HALF:I]).then_inc(s_raw[1][kind], 16)
            sp.dma_start(raw_view(1, DOWN), shared_rows[DOWN][:, IC:2 * IC, :]).then_inc(s_raw[1][DOWN], 16)
            for m in range(6):
                sp.wait_ge(s_w_lo, m + 1)
                load_piece(m, e_a)
            e_next = pick(1, 0)
            sp.wait_ge(s_tr, batch(0, X_BATCH) + 1)
            load_x(1)
            for kind, last in ((UP, UP_BATCH + 1), (GATE, GATE_BATCH + 1), (DOWN, DOWN_BATCH + 1)):
                sp.wait_ge(s_tr, batch(0, last) + 1)
                load_layer0(kind, e_next)
            for m in (6, 7):
                sp.wait_ge(s_w_lo, piece(0, m - 6) + 1)
                load_piece(m, e_b)

            def store(b):
                sp.wait_ge(s_free[0], b + 2)
                sp.wait_ge(s_free[1], b + 2)
                sp.dma_start(out_rows[bass.ds(b, 1)].rearrange("o p c d -> (o p) c d"), y[:, :, :]).then_inc(s_out, 16)

            def rest_of_b(b):
                e = pick(b, 1)
                for m in range(8, PIECES):
                    sp.wait_ge(s_w_lo, piece(b, m - 6) + 1)
                    load_piece(m, e)

            def sample(b, layer0):
                rest_of_b(b)
                if layer0:
                    e0 = pick(b + 2, 0)
                    sp.wait_ge(s_tr, batch(b + 1, X_BATCH) + 1)
                    load_x(b + 2)
                    sp.wait_ge(s_tr, batch(b + 1, UP_BATCH + 1) + 1)
                    load_layer0(UP, e0)
                    sp.wait_ge(s_tr, batch(b + 1, GATE_BATCH + 1) + 1)
                    load_layer0(GATE, e0)
                    sp.wait_ge(s_tr, batch(b + 1, DOWN_BATCH + 1) + 1)
                    load_layer0(DOWN, e0)
                e_first = pick(b + 1, 0)
                for m in range(6):
                    sp.wait_ge(s_w_lo, piece(b, m + 6) + 1)
                    load_piece(m, e_first)
                e_second = pick(b + 1, 1)
                for m in (6, 7):
                    sp.wait_ge(s_w_lo, piece(b + 1, m - 6) + 1)
                    load_piece(m, e_second)
                store(b)

            with sp.Fori(0, B - 2) as b:
                sample(b, True)
            sample(B - 2, False)
            rest_of_b(B - 1)
            store(B - 1)
            sp.wait_ge(s_out, 16 * (B + 1))

        @block.gpsimd
        def _(pool):
            pool.sem_inc(s_out, 16)
            nc.gpsimd.memset(ident[:, :], 0.0).then_inc(s_ident0, 1)
            nc.gpsimd.memset(ones[:, :], 1.0).then_inc(s_ident, 1)
            pool.wait_ge(s_ident0, 1)
            nc.gpsimd.affine_select(out=ident[:, :], in_=ident[:, :], compare_op=ALU.not_equal, fill=1.0,
                                    base=0, pattern=[[-1, P]], channel_multiplier=1).then_inc(s_ident, 1)

        @block.scalar
        def _(act):
            def split_hi(b, m, place, nth):
                h, kind = m // 3 % 4, m % 3
                act.wait_ge(s_raw[h % 2][kind], 16 * nth)
                nc.scalar.activation(w_hi[place][kind][:, :], raw[h % 2][kind][:, :], ACT.Copy).then_inc(s_w_hi, 1)

            def split_hi_shared(m):
                split_hi(0, m, 2 + m // 3, 1)

            def split_hi_routed(b, m):
                if m >= PIECES:
                    b, m = b + 1, m - PIECES
                split_hi(b, m, m // 3 % 2, 2 * b + m // 6 + 2)

            def transposed_hi(s, i):
                act.wait_ge(s_tr, batch(s, i) + 1)
                ps = tr_ps[i % 2][:, :, :].rearrange("p a b -> p (a b)")
                if i == X_BATCH:
                    nc.scalar.activation(xT[:, :, :].rearrange("p a b -> p (a b)"), ps, ACT.Copy)
                    dst = xT_hi[:, :, :].rearrange("p a b -> p (a b)")
                elif i < GATE_BATCH:
                    dst = up0_hi[:, i - UP_BATCH, :]
                elif i < DOWN_BATCH:
                    dst = gate0_hi[:, i - GATE_BATCH, :]
                else:
                    k = 2 * (i - DOWN_BATCH)
                    dst = down0_hi[:, k:k + 2, :].rearrange("p a b -> p (a b)")
                nc.scalar.activation(dst, ps, ACT.Copy).then_inc(s_tr_hi, 1)

            def activate(n, r, kind, k, e):
                act.wait_ge(s_gu, n + 1)
                if kind == "L":
                    for c in range(2):
                        ins = nc.scalar.activation(act_out[:, r, c, :], up_ps[r][:, c, :], ACT.Silu,
                                                   bias=bias_up[:, bass.ds(e * HC + 2 * k + c, 1)])
                    ins.then_inc(s_act, 1)
                else:
                    nc.scalar.activation(act_out[:, r, :, :].rearrange("p a b -> p (a b)"),
                                         gate_ps[r][:, :, :].rearrange("p a b -> p (a b)"),
                                         ACT.Gelu_apprx_tanh).then_inc(s_act, 1)

            def hidden_hi(n, r, used=True):
                act.wait_ge(s_mul, n + 1)
                if used:
                    act.wait_ge(s_down, n - 1)
                nc.scalar.activation(h_hi[r][:, :, :].rearrange("p a b -> p (a b)"),
                                     hidden[:, r, :, :].rearrange("p a b -> p (a b)"), ACT.Copy).then_inc(s_h_hi, 1)

            def next_x1_hi(s):
                act.wait_ge(s_x1T, s + 1)
                nc.scalar.activation(x1_hi[:, :, :].rearrange("p a b -> p (a b)"),
                                     x1T[:, :, :].rearrange("p a b -> p (a b)"), ACT.Copy).then_inc(s_x1_hi, 1)

            def evacuate(b, n_last):
                act.wait_ge(s_down, n_last + 1)
                act.wait_ge(s_out, 16 * (b + 1))
                nc.scalar.activation(y[:, 0, :], out_ps[0][:, 0:D], ACT.Copy).then_inc(s_free[0], 1)

            def pick(s):
                return act.value_load(expert[0:1, bass.ds(s, 1), 0:1].rearrange("p a b -> p (a b)"),
                                      min_val=0, max_val=E - 1)

            act.wait_ge(s_top, 1)
            nc.scalar.activation(exps[:, :], top[:, :], ACT.Exp, bias=neg_max[:, 0:1],
                                 accum_out=exp_sum[:, 0:1]).then_inc(s_exp, 1)
            act.wait_ge(s_ident, 2)
            nc.scalar.activation(ident_r[:, :], ident[:, :], ACT.Copy).then_inc(s_identr, 1)

            transposed_hi(0, X_BATCH)
            split_hi_shared(0)
            split_hi_shared(1)
            act.wait_ge(s_free[0], 1)
            e0 = pick(0)
            for i in range(1, BATCHES):
                transposed_hi(0, i)
            split_hi_shared(2)
            for k in range(2):
                activate(k, k, "L", k, e0)
                split_hi_shared(3 + k)
                hidden_hi(k, k, used=False)
            split_hi_shared(5)
            next_x1_hi(0)
            for m in range(EARLY_PIECES):
                split_hi_routed(0, m)

            with act.Fori(0, B - 1) as b:
                e0 = pick(b + 1)
                for j, (kind, k) in enumerate(PLAN):
                    n = position(b, j)
                    activate(n, j % 2, kind, k, e0)
                    if j == NPOS - 1:
                        next_x1_hi(b + 1)
                    if j < BATCHES:
                        transposed_hi(b + 1, j)
                    for m in SPLIT_AT.get(j, ()):
                        split_hi_routed(b, m)
                    hidden_hi(n, j % 2)
                evacuate(b, position(b, NPOS - 1))
            b = B - 1
            for j, (kind, k) in enumerate(LAST_PLAN):
                n = position(b, j)
                activate(n, j % 2, kind, k, None)
                for m in LAST_SPLIT_AT.get(j, ()):
                    split_hi_routed(b, m)
                hidden_hi(n, j % 2)
            evacuate(b, position(b, len(LAST_PLAN) - 1))

        @block.vector
        def _(dve):
            def split_lo(m, place, number):
                h, kind = m // 3 % 4, m % 3
                dve.wait_ge(s_w_hi, number + 1)
                nc.vector.tensor_tensor(w_lo[place][kind][:, :], raw[h % 2][kind][:, :],
                                        w_hi[place][kind][:, :].bitcast(F32), ALU.subtract).then_inc(s_w_lo, 1)

            def split_lo_shared(m):
                split_lo(m, 2 + m // 3, m)

            def split_lo_routed(b, m):
                if m >= PIECES:
                    b, m = b + 1, m - PIECES
                split_lo(m, m // 3 % 2, piece(b, m))

            def transposed_lo(s, i):
                dve.wait_ge(s_tr_hi, batch(s, i) + 1)
                if i == X_BATCH:
                    hi, lo = (t[:, :, :].rearrange("p a b -> p (a b)") for t in (xT_hi, xT_lo))
                elif i < GATE_BATCH:
                    hi, lo = (t[:, i - UP_BATCH, :] for t in (up0_hi, up0_lo))
                elif i < DOWN_BATCH:
                    hi, lo = (t[:, i - GATE_BATCH, :] for t in (gate0_hi, gate0_lo))
                else:
                    k = 2 * (i - DOWN_BATCH)
                    hi, lo = (t[:, k:k + 2, :].rearrange("p a b -> p (a b)") for t in (down0_hi, down0_lo))
                nc.vector.tensor_tensor(lo, tr_ps[i % 2][:, :, :].rearrange("p a b -> p (a b)"),
                                        hi.bitcast(F32), ALU.subtract).then_inc(s_tr_lo, 1)

            def multiply(n, r, kind, k, b, e):
                dve.wait_ge(s_act, n + 1)
                flat = "p a b -> p (a b)"
                if kind == "L":
                    for c in range(2):
                        ins = nc.vector.scalar_tensor_tensor(
                            out=hidden[:, r, c, :], in0=gate_ps[r][:, c, :],
                            scalar=bias_gate[:, bass.ds(e * HC + 2 * k + c, 1)], in1=act_out[:, r, c, :],
                            op0=ALU.add, op1=ALU.mult)
                    ins.then_inc(s_mul, 1)
                elif kind == "S":
                    nc.vector.tensor_tensor(hidden[:, r, :, :].rearrange(flat), up_ps[r][:, :, :].rearrange(flat),
                                            act_out[:, r, :, :].rearrange(flat), ALU.mult).then_inc(s_mul, 1)
                else:
                    nc.vector.scalar_tensor_tensor(
                        out=hidden[:, r, :, :].rearrange(flat), in0=act_out[:, r, :, :].rearrange(flat),
                        scalar=route[:, bass.ds(b, 1), "AB".index(kind):"AB".index(kind) + 1].rearrange(flat),
                        in1=up_ps[r][:, :, :].rearrange(flat), op0=ALU.mult, op1=ALU.mult).then_inc(s_mul, 1)

            def hidden_lo(n, r):
                dve.wait_ge(s_h_hi, n + 1)
                flat = "p a b -> p (a b)"
                nc.vector.tensor_tensor(h_lo[r][:, :, :].rearrange(flat), hidden[:, r, :, :].rearrange(flat),
                                        h_hi[r][:, :, :].rearrange(flat).bitcast(F32), ALU.subtract).then_inc(s_h_lo, 1)

            def next_x1T(s, n, e):
                dve.wait_ge(s_down, n + 1)
                for dc in range(DC):
                    ins = nc.vector.scalar_tensor_tensor(
                        out=x1T[:, dc, :], in0=tr_ps[dc][:, 0:SC, :].rearrange("p a b -> p (a b)"),
                        scalar=bias_down[:, bass.ds(e * DC + dc, 1)],
                        in1=xT[:, dc, :], op0=ALU.add, op1=ALU.add)
                ins.then_inc(s_x1T, 1)

            def next_x1_lo(s):
                dve.wait_ge(s_x1_hi, s + 1)
                flat = "p a b -> p (a b)"
                nc.vector.tensor_tensor(x1_lo[:, :, :].rearrange(flat), x1T[:, :, :].rearrange(flat),
                                        x1_hi[:, :, :].rearrange(flat).bitcast(F32), ALU.subtract).then_inc(s_x1_lo, 1)

            def evacuate(b, n_last):
                dve.wait_ge(s_down, n_last + 1)
                dve.wait_ge(s_out, 16 * (b + 1))
                nc.vector.tensor_copy(y[:, 1, :], out_ps[1][:, 0:D]).then_inc(s_free[1], 1)

            def pick(s):
                return dve.value_load(expert[0:1, bass.ds(s, 1), 0:1].rearrange("p a b -> p (a b)"),
                                      min_val=0, max_val=E - 1)

            links = [0]

            def chained(ins):
                links[0] += 1
                ins.then_inc(s_chain, 1)
                dve.wait_ge(s_chain, links[0])

            dve.wait_ge(s_cond, 16)
            chained(nc.vector.max(top[:, :], logits[:, :]))
            nc.vector.tensor_scalar(neg_max[:, :], top[:, 0:1], -1.0, None, ALU.mult).then_inc(s_top, 1)
            chained(nc.vector.max_index(top_at[:, :], top[:, :], logits[:, :]))
            nc.vector.tensor_copy(choice[:, 2:4], top_at[:, 0:2])
            dve.wait_ge(s_exp, 1)
            chained(nc.vector.reciprocal(exp_inv[:, :], exp_sum[:, :]))
            chained(nc.vector.tensor_scalar(probs[:, :], exps[:, 0:2], exp_inv[:, 0:1], None, ALU.mult))
            chained(nc.vector.tensor_tensor(pair_sum[:, :], probs[:, 0:1], probs[:, 1:2], ALU.add))
            chained(nc.vector.reciprocal(pair_inv[:, :], pair_sum[:, :]))
            chained(nc.vector.tensor_scalar(pair_w[:, :], probs[:, :], pair_inv[:, 0:1], None, ALU.mult))
            chained(nc.vector.tensor_scalar(pair_w2[:, :], pair_w[:, :], 1.0 - MIX, None, ALU.mult))
            chained(nc.vector.scalar_tensor_tensor(out=choice[:, 0:2], in0=pair_w[:, :], scalar=MIX, in1=pair_w2[:, :],
                                                   op0=ALU.mult, op1=ALU.add))
            dve.wait_ge(s_ident, 2)
            nc.vector.tensor_tensor(choice_diag[:, :, :],
                                    choice[:, :].rearrange("p (o c) -> p o c", o=1).to_broadcast([B, B, 4]),
                                    ident[0:B, 0:B].rearrange("p (b o) -> p b o", o=1).to_broadcast([B, B, 4]),
                                    ALU.mult).then_inc(s_diag, 1)
            dve.wait_ge(s_spread, 1)
            spread = out_ps[0][:, 0:4 * B].rearrange("p (b c) -> p b c", c=4)
            nc.vector.tensor_copy(route[:, :, :], spread)
            nc.vector.tensor_copy(expert[:, :, :], spread[:, :, 2:4]).then_inc(s_free[0], 1)
            dve.wait_ge(s_biasT, 1)
            nc.vector.tensor_copy(bias_up[:, :], out_ps[1][:, 0:E * HC])
            nc.vector.tensor_copy(bias_gate[:, :], out_ps[1][:, P:P + E * HC])
            nc.vector.tensor_copy(bias_down[:, :], out_ps[1][:, 2 * P:2 * P + E * DC]).then_inc(s_free[1], 1)

            dve.wait_ge(s_free[0], 1)
            dve.wait_ge(s_free[1], 1)
            e0 = pick(0)
            transposed_lo(0, X_BATCH)
            split_lo_shared(0)
            split_lo_shared(1)
            for i in range(1, BATCHES):
                transposed_lo(0, i)
            split_lo_shared(2)
            for k in range(2):
                multiply(k, k, "L", k, None, e0)
                split_lo_shared(3 + k)
                hidden_lo(k, k)
            split_lo_shared(5)
            next_x1T(0, 1, e0)
            next_x1_lo(0)
            for m in range(EARLY_PIECES):
                split_lo_routed(0, m)

            x1_at = PLAN.index(("L", 1)) + LAG + 1
            with dve.Fori(0, B - 1) as b:
                e0 = pick(b + 1)
                for j, (kind, k) in enumerate(PLAN):
                    n = position(b, j)
                    if j == x1_at:
                        next_x1T(b + 1, position(b, j - LAG - 1), e0)
                    multiply(n, j % 2, kind, k, b, e0)
                    if j == NPOS - 1:
                        next_x1_lo(b + 1)
                    if j < BATCHES:
                        transposed_lo(b + 1, j)
                    for m in SPLIT_AT.get(j, ()):
                        split_lo_routed(b, m)
                    hidden_lo(n, j % 2)
                evacuate(b, position(b, NPOS - 1))
            b = B - 1
            for j, (kind, k) in enumerate(LAST_PLAN):
                n = position(b, j)
                multiply(n, j % 2, kind, k, b, None)
                for m in LAST_SPLIT_AT.get(j, ()):
                    split_lo_routed(b, m)
                hidden_lo(n, j % 2)
            evacuate(b, position(b, len(LAST_PLAN) - 1))

        @block.tensor
        def _(pe):
            def three_passes(ps, w, m, first, last):
                nc.tensor.matmul(ps, w[0], m[0], start=first, stop=False)
                nc.tensor.matmul(ps, w[0], m[1], start=False, stop=False)
                return nc.tensor.matmul(ps, w[1], m[0], start=False, stop=last)

            def gate_up(n, r, kind, k):
                pe.wait_ge(s_mul, n - 1)
                for c in range(2):
                    for ps, what in ((gate_ps, GATE), (up_ps, UP)):
                        for dc in range(DC):
                            if kind == "L":
                                col = slice((2 * k + c) * P, (2 * k + c + 1) * P)
                                hi, lo = (gate0_hi, gate0_lo) if what == GATE else (up0_hi, up0_lo)
                                w = hi[:, dc, col], lo[:, dc, col]
                                m = xT_hi[:, dc, :], xT_lo[:, dc, :]
                            else:
                                w = chunk(half_of(kind, k), what, dc, 2 * (k % 2) + c)
                                m = x1_hi[:, dc, :], x1_lo[:, dc, :]
                            ins = three_passes(ps[r][:, c, :], w, m, dc == 0, dc == DC - 1)
                ins.then_inc(s_gu, 1)

            def down(n, r, kind, k, first, last):
                pe.wait_ge(s_h_lo, n + 1)
                if kind == "L":
                    for c in range(2):
                        hc = 2 * k + c
                        for dc in range(DC):
                            col = slice(dc * P, (dc + 1) * P)
                            ins = three_passes(tr_ps[dc][:, 0:SC, :].rearrange("p a b -> p (a b)"),
                                               (down0_hi[:, hc, col], down0_lo[:, hc, col]),
                                               (h_hi[r][:, c, :], h_lo[r][:, c, :]),
                                               hc == 0, hc == HC - 1)
                else:
                    if first:
                        for sc in range(SC):
                            for dc in range(DC):
                                for part in (x1_hi, x1_lo):
                                    nc.tensor.matmul(out_ps[sc][:, dc * P:(dc + 1) * P],
                                                     part[:, dc, sc * P:(sc + 1) * P], ident_r[:, :],
                                                     start=(dc == 0 and part is x1_hi), stop=False,
                                                     skip_group_check=True)
                    place = half_of(kind, k)
                    for c in range(2):
                        at = (2 * (k % 2) + c) * D
                        w = w_hi[place][DOWN][:, at:at + D], w_lo[place][DOWN][:, at:at + D]
                        for sc in range(SC):
                            col = slice(sc * P, (sc + 1) * P)
                            h = h_hi[r][:, c, col], h_lo[r][:, c, col]
                            ps = out_ps[sc][:, 0:D]
                            for a, (i1, i2) in enumerate(((0, 0), (0, 1), (1, 0))):
                                ins = nc.tensor.matmul(ps, h[i1], w[i2], start=False,
                                                       stop=(last and c == 1 and a == 2), skip_group_check=True)
                ins.then_inc(s_down, 1)

            def transpose_batch(s, i):
                if i == X_BATCH:
                    pe.wait_ge(s_x, 16 * (s + 1))
                    blocks = [x_raw[:, sc, dc * P:(dc + 1) * P] for dc in range(DC) for sc in range(SC)]
                elif i < GATE_BATCH:
                    pe.wait_ge(s_w0[UP], 16 * (s + 1))
                    dc = i - UP_BATCH
                    blocks = [up0_raw[:, hc, dc * P:(dc + 1) * P] for hc in range(HC)]
                elif i < DOWN_BATCH:
                    pe.wait_ge(s_w0[GATE], 16 * (s + 1))
                    dc = i - GATE_BATCH
                    blocks = [gate0_raw[:, hc, dc * P:(dc + 1) * P] for hc in range(HC)]
                else:
                    pe.wait_ge(s_w0[DOWN], 16 * (s + 1))
                    k = 2 * (i - DOWN_BATCH)
                    blocks = [down0_raw[:, dc, hc * P:(hc + 1) * P] for hc in (k, k + 1) for dc in range(DC)]
                if i >= 2:
                    pe.wait_ge(s_tr_lo, batch(s, i - 2) + 1)
                else:
                    pe.wait_ge(s_x1T, s)
                for c, blk in enumerate(blocks):
                    ins = nc.tensor.transpose(tr_ps[i % 2][:, c, :], blk, ident[:, :])
                ins.then_inc(s_tr, 1)

            pe.wait_ge(s_ident, 2)
            pe.wait_ge(s_bias, 48)
            for c in range(2):
                nc.tensor.transpose(out_ps[1][:, c * P:c * P + E * HC], bias_rows[:, c, :], ident[0:E * HC, 0:E * HC])
            nc.tensor.transpose(out_ps[1][:, 2 * P:2 * P + E * DC], bias_down_rows[:, :],
                                ident[0:E * DC, 0:E * DC]).then_inc(s_biasT, 1)
            transpose_batch(0, X_BATCH)
            pe.wait_ge(s_diag, 1)
            nc.tensor.matmul(out_ps[0][:, 0:4 * B], ones[:, :], choice_diag[:, :, :].rearrange("p a b -> p (a b)"),
                             start=True, stop=True).then_inc(s_spread, 1)
            for i in range(1, BATCHES):
                transpose_batch(0, i)
            pe.wait_ge(s_tr_lo, batch(0, DOWN_BATCH + 1) + 1)
            for k in range(2):
                for c in range(1):
                    gate_up_first(pe, nc, k, three_passes, gate_ps, up_ps, gate0_hi, gate0_lo, up0_hi, up0_lo,
                                  xT_hi, xT_lo, DC).then_inc(s_gu, 1)
            for k in range(2):
                down(k, k, "L", k, False, False)
            pe.wait_ge(s_identr, 1)
            pe.wait_ge(s_w_lo, 2)

            def sample(b, plan, layer0):
                steps = len(plan)
                pe.wait_ge(s_x1_lo, b + 1)
                for j in range(steps + LAG):
                    if j < steps:
                        kind, k = plan[j]
                        if kind in "AB" and k % 2 == 0:
                            pe.wait_ge(s_w_lo, piece(b, 6 * (kind == "B") + 3 * (k // 2) + UP) + 1)
                        if kind == "L" and k == 0:
                            pe.wait_ge(s_tr_lo, batch(b + 1, DOWN_BATCH + 1) + 1)
                        gate_up(position(b, j), j % 2, kind, k)
                        if layer0 and j < BATCHES:
                            transpose_batch(b + 1, j)
                    if j >= LAG:
                        kind, k = plan[j - LAG]
                        if kind in "AB" and k % 2 == 0:
                            pe.wait_ge(s_w_lo, piece(b, 6 * (kind == "B") + 3 * (k // 2) + DOWN) + 1)
                        if j == LAG:
                            pe.wait_ge(s_free[0], b + 1)
                            pe.wait_ge(s_free[1], b + 1)
                        down(position(b, j - LAG), j % 2, kind, k, j == LAG, j == steps + LAG - 1)

            with pe.Fori(0, B - 1) as b:
                sample(b, PLAN, True)
            sample(B - 1, LAST_PLAN, False)


def gate_up_first(pe, nc, k, three_passes, gate_ps, up_ps, gate0_hi, gate0_lo, up0_hi, up0_lo, xT_hi, xT_lo, DC):
    for c in range(2):
        col = slice((2 * k + c) * P, (2 * k + c + 1) * P)
        for ps, hi, lo in ((gate_ps, gate0_hi, gate0_lo), (up_ps, up0_hi, up0_lo)):
            for dc in range(DC):
                ins = three_passes(ps[k][:, c, :], (hi[:, dc, col], lo[:, dc, col]),
                                   (xT_hi[:, dc, :], xT_lo[:, dc, :]), dc == 0, dc == DC - 1)
    return ins


_INS = ['x', 'cond_8', 'L0_cond_W_up', 'L0_cond_b_up', 'L0_cond_W_gate', 'L0_cond_b_gate', 'L0_cond_W_down',
        'L0_cond_b_down', 'L1_cond_skill_gate', 'L1_cond_skill_up', 'L1_cond_skill_down', 'L1_cond_shared_gate',
        'L1_cond_shared_up', 'L1_cond_shared_down']


def kernel(**inputs):
    import numpy as _np
    import concourse.bacc as _bacc
    from concourse import mybir as _mybir
    from concourse.bass_utils import run_bass_kernel_spmd as _run

    nc = _bacc.Bacc("TRN2", target_bir_lowering=False, num_devices=1)
    arrays, args = {}, []
    for name in _INS:
        a = _np.ascontiguousarray(inputs[name])
        arrays[f"in_{name}_dram"] = a
        args.append(nc.dram_tensor(f"in_{name}_dram", a.shape, _mybir.dt.from_np(a.dtype), kind="ExternalInput").ap())
    shape = arrays["in_x_dram"].shape
    args.append(nc.dram_tensor("out_dram", shape, _mybir.dt.float32, kind="ExternalOutput").ap())
    bass_cond_two_layer_kernel(nc, *args)
    r = _run(nc, [arrays], core_ids=[0])
    return r.results[0]["out_dram"]
```

```python
from contextlib import ExitStack

import concourse.bass as bass
from concourse import mybir

P = 128
ALU = mybir.AluOpType
ACT = mybir.ActivationFunctionType
F32 = mybir.dt.float32
F32R = mybir.dt.float32r
I32 = mybir.dt.int32
U32 = mybir.dt.uint32

NUM_MOE_LAYERS = 12
MIX = 1.0 / NUM_MOE_LAYERS

PLAN = [("S", 0), ("S", 1), ("A", 0), ("A", 1), ("S", 2), ("A", 2), ("A", 3),
        ("L", 0), ("L", 1), ("B", 0), ("B", 1), ("S", 3), ("B", 2), ("B", 3)]
LAST_PLAN = [step for step in PLAN if step[0] != "L"]
NPOS = len(PLAN)
LAG = 2

GATE, UP, DOWN = range(3)
PIECES = 12
SPLIT_AT = {0: [2], 1: [3], 2: [4], 3: [5], 5: [6], 6: [7], 7: [8], 8: [9], 9: [10], 10: [11], 11: [12]}
LAST_SPLIT_AT = {0: [2], 1: [3], 2: [4], 3: [5], 4: [6], 5: [7], 6: [8], 7: [9], 8: [10], 9: [11]}
AHEAD = 1
SHARED_PIECES = 6

BLK = 32
X_BATCH, UP_BATCH, GATE_BATCH, DOWN_BATCH = 0, 1, 3, 5
BATCHES = 7
BATCH_AT = {0: 0, 1: 1, 2: 2, 3: 3, 4: 4, 6: 5, 7: 6}


def bass_cond_two_layer_kernel(
    nc: bass.Bass,
    x: bass.AP,
    cond: bass.AP,
    up0_w: bass.AP,
    up0_b: bass.AP,
    gate0_w: bass.AP,
    gate0_b: bass.AP,
    down0_w: bass.AP,
    down0_b: bass.AP,
    skill_gate: bass.AP,
    skill_up: bass.AP,
    skill_down: bass.AP,
    shared_gate: bass.AP,
    shared_up: bass.AP,
    shared_down: bass.AP,
    out: bass.AP,
):
    B, S, D = x.shape
    E, H = up0_b.shape
    I = shared_gate.shape[1]
    SC, DC, HC = S // P, D // P, H // P
    HALF = I // 2
    IC = HALF // P
    assert (SC, DC, HC, IC) == (2, 2, 4, 4) and cond.shape == (B, E) and E == 8
    Q = P // BLK
    DQ, HQ = D // Q, H // Q

    def position(b, j):
        return 2 + NPOS * b + j

    def piece(b, m):
        return SHARED_PIECES + PIECES * b + m

    def batch(s, i):
        return BATCHES * s + i

    ctx = ExitStack()
    with ctx:
        def sb(name, shape, dt=F32):
            return ctx.enter_context(nc.sbuf_tensor(name, shape, dt))

        def bank(name, shape):
            return ctx.enter_context(nc.psum_tensor(name, shape, F32))

        def sem(name):
            return ctx.enter_context(nc.semaphore(name))

        ident = sb("ident", [P, P])
        ones = sb("ones", [B, P])
        logits = sb("logits", [B, E])
        top = sb("top", [B, 8])
        top_at = sb("top_at", [B, 8], U32)
        neg_max = sb("neg_max", [B, 1])
        exps = sb("exps", [B, 8])
        exp_sum = sb("exp_sum", [B, 1])
        exp_inv = sb("exp_inv", [B, 1])
        probs = sb("probs", [B, 2])
        pair_sum = sb("pair_sum", [B, 1])
        pair_inv = sb("pair_inv", [B, 1])
        pair_w = sb("pair_w", [B, 2])
        pair_w2 = sb("pair_w2", [B, 2])
        choice = sb("choice", [B, 2])
        choice_diag = sb("choice_diag", [B, B, 2])
        weight = sb("weight", [B, 2])
        weight_diag = sb("weight_diag", [B, B, 2])
        route = sb("route", [P, B, 2])
        expert = sb("expert", [P, B, 2], I32)
        bias_rows = sb("bias_rows", [E * HC, 2, P])
        bias_down_rows = sb("bias_down_rows", [E, D])
        bias_up = sb("bias_up", [P, E * HC])
        bias_gate = sb("bias_gate", [P, E * HC])
        bias_down = sb("bias_down", [P, E * DC])

        x_raw = sb("x_raw", [P, S // BLK, DQ])
        up0_raw = sb("up0_raw", [P, H // BLK, DQ])
        gate0_raw = sb("gate0_raw", [P, H // BLK, DQ])
        down0_raw = sb("down0_raw", [P, D // BLK, HQ])
        turned = [sb(f"turned{r}", [P, H]) for r in range(2)]
        xT = sb("xT", [P, DC, S])
        xT_hi, xT_lo = sb("xT_hi", [P, DC, S], F32R), sb("xT_lo", [P, DC, S], F32R)
        up0_hi, up0_lo = sb("up0_hi", [P, DC, H], F32R), sb("up0_lo", [P, DC, H], F32R)
        gate0_hi, gate0_lo = sb("gate0_hi", [P, DC, H], F32R), sb("gate0_lo", [P, DC, H], F32R)
        down0_hi, down0_lo = sb("down0_hi", [P, HC, D], F32R), sb("down0_lo", [P, HC, D], F32R)

        x1T = sb("x1T", [P, DC, S])
        x1_hi, x1_lo = sb("x1_hi", [P, DC, S], F32R), sb("x1_lo", [P, DC, S], F32R)
        raw = [[sb(f"raw{r}_{k}", [P, DC * HALF]) for k in ("gate", "up", "down")] for r in range(2)]
        w_hi = [[sb(f"w_hi{r}_{k}", [P, DC * HALF], F32R) for k in ("gate", "up", "down")] for r in range(4)]
        w_lo = [[sb(f"w_lo{r}_{k}", [P, DC * HALF], F32R) for k in ("gate", "up", "down")] for r in range(4)]

        act_out = sb("act_out", [P, 2, 2, S])
        hidden = sb("hidden", [P, 2, 2, S])
        h_hi = [sb(f"h_hi{r}", [P, 2, S], F32R) for r in range(2)]
        h_lo = [sb(f"h_lo{r}", [P, 2, S], F32R) for r in range(2)]
        y = sb("y", [P, SC, D])

        gate_ps = [bank(f"gate_ps{r}", [P, 2, S]) for r in range(2)]
        up_ps = [bank(f"up_ps{r}", [P, 2, S]) for r in range(2)]
        sum0_ps = [bank(f"sum0_ps{r}", [P, 512]) for r in range(2)]
        out_ps = [bank(f"out_ps{r}", [P, 512]) for r in range(2)]

        s_ident0 = sem("ident_zeroed")
        s_ident = sem("ident_ready")
        s_cond = sem("cond_loaded")
        s_bias = sem("bias_loaded")
        s_chain = sem("vector_chain")
        s_top = sem("top_ready")
        s_exp = sem("exps_ready")
        s_diag = sem("choice_diag_ready")
        s_spread = sem("choices_spread")
        s_wdiag = sem("weight_diag_ready")
        s_wspread = sem("weights_spread")
        s_expert = sem("experts_ready")
        s_biasT = sem("bias_transposed")
        s_x = sem("x_loaded")
        s_w0 = [sem(f"layer0_{k}_loaded") for k in ("gate", "up", "down")]
        s_raw = [[sem(f"raw{r}_{k}_loaded") for k in ("gate", "up", "down")] for r in range(2)]
        s_tr = sem("batch_transposed")
        s_tr_hi = sem("batch_hi_ready")
        s_tr_lo = sem("batch_lo_ready")
        s_w_hi = sem("piece_hi_ready")
        s_w_lo = sem("piece_lo_ready")
        s_gu = sem("gate_up_done")
        s_act = sem("act_done")
        s_mul = sem("hidden_done")
        s_h_hi = sem("hidden_hi_ready")
        s_h_lo = sem("hidden_lo_ready")
        s_down = sem("down_done")
        s_act_c0 = sem("last_act_chunk0_done")
        s_mul_c0 = sem("last_hidden_chunk0_done")
        s_h_hi_c0 = sem("last_hidden_chunk0_hi_ready")
        s_h_lo_c0 = sem("last_hidden_chunk0_lo_ready")
        s_x1T = sem("x1T_ready")
        s_x1_hi = sem("x1_hi_ready")
        s_x1_lo = sem("x1_lo_ready")
        s_free = [sem(f"out_bank{r}_read") for r in range(2)]
        s_out = sem("out_stored")

        def half_of(kind, k):
            return k // 2 + (2 if kind == "S" else 0)

        def chunk(r, kind, dc, ic):
            c = dc * HALF + ic * P
            return w_hi[r][kind][:, c:c + P], w_lo[r][kind][:, c:c + P]

        def raw_order(t, kind):
            return t[:, :].rearrange("p (k a c) -> p k c a", c=DC, a=P) if kind == DOWN else t[:, :]

        def split_view(t, kind):
            return t[:, :].rearrange("p (k c a) -> p k c a", c=DC, a=P) if kind == DOWN else t[:, :]

        def sum_cols(sc):
            return out_ps[sc][:, 0:D].rearrange("p (c a) -> p c a", c=DC)

        def y_cols(sc):
            return y[:, sc, :].rearrange("p (a c) -> p c a", c=DC)

        def batch_views(i):
            flat = "p a b -> p (a b)"
            if i == X_BATCH:
                return tuple(t[:, :, :].rearrange(flat) for t in (xT, xT_hi, xT_lo))
            t = turned[i % 2]
            if i < GATE_BATCH:
                return t[:, :], up0_hi[:, i - UP_BATCH, :], up0_lo[:, i - UP_BATCH, :]
            if i < DOWN_BATCH:
                return t[:, :], gate0_hi[:, i - GATE_BATCH, :], gate0_lo[:, i - GATE_BATCH, :]
            k = 2 * (i - DOWN_BATCH)
            return (t[:, :].rearrange("p (k a c) -> p k c a", c=DC, a=P),
                    down0_hi[:, k:k + 2, :].rearrange("p k (c a) -> p k c a", c=DC),
                    down0_lo[:, k:k + 2, :].rearrange("p k (c a) -> p k c a", c=DC))

        def loop(eng, count):
            return nc.Fori(0, count, engines=(eng.engine,), hint_back_edge=True)

        block = ctx.enter_context(nc.Block())

        @block.sync
        def _(sp):
            out_rows = out.rearrange("b (c p) d -> b p c d", c=SC)
            x_blocks = x.rearrange("b (n r) (q k) -> b q r n k", r=BLK, q=Q)
            layer0_blocks = [gate0_w.rearrange("e (n r) (q k) -> e q r n k", r=BLK, q=Q),
                             up0_w.rearrange("e (n r) (q k) -> e q r n k", r=BLK, q=Q),
                             down0_w.rearrange("e (n r) (q k) -> e q r n k", r=BLK, q=Q)]
            layer0_raw = [gate0_raw, up0_raw, down0_raw]
            skill_rows = [skill_gate.rearrange("e (p c) i -> e p c i", p=P),
                          skill_up.rearrange("e (p c) i -> e p c i", p=P),
                          skill_down.rearrange("e (c p) d -> e p c d", p=P)]
            shared_rows = [shared_gate.rearrange("(p c) i -> p c i", p=P),
                           shared_up.rearrange("(p c) i -> p c i", p=P),
                           shared_down.rearrange("(c p) d -> p c d", p=P)]

            def raw_view(r, kind):
                return raw[r][kind][:, :].rearrange("p (c n) -> p c n", c=(IC if kind == DOWN else DC))

            def load_blocks(raw, blocks, at, loaded):
                for q in range(Q):
                    sp.dma_start(raw[q * BLK:(q + 1) * BLK, :, :],
                                 blocks[bass.ds(at, 1), q].rearrange("o r n k -> (o r) n k")).then_inc(loaded, 16)

            def load_x(s):
                load_blocks(x_raw, x_blocks, s, s_x)

            def load_layer0(kind, e):
                load_blocks(layer0_raw[kind], layer0_blocks[kind], e, s_w0[kind])

            def load_piece(m, e):
                h, kind = m // 3, m % 3
                k = h % 2
                rows = skill_rows[kind][bass.ds(e, 1)].rearrange("o p c n -> (o p) c n")
                part = rows[:, k * IC:(k + 1) * IC, :] if kind == DOWN else rows[:, :, k * HALF:(k + 1) * HALF]
                sp.dma_start(raw_view(h % 2, kind), part).then_inc(s_raw[h % 2][kind], 16)

            def pick(s, choice_no):
                return sp.value_load(expert[0:1, bass.ds(s, 1), choice_no:choice_no + 1].rearrange("p a b -> p (a b)"),
                                     min_val=0, max_val=E - 1)

            sp.dma_start(logits[:, :], cond[:, :]).then_inc(s_cond, 16)
            load_x(0)
            sp.dma_start(raw_view(0, GATE), shared_rows[GATE][:, :, 0:HALF]).then_inc(s_raw[0][GATE], 16)
            sp.wait_ge(s_expert, 1)
            e_a = pick(0, 0)
            for kind in (UP, GATE, DOWN):
                load_layer0(kind, e_a)
            for k, bias in enumerate((up0_b, gate0_b)):
                for q in range(Q):
                    sp.dma_start(bias_rows[:, k, q * BLK:(q + 1) * BLK],
                                 bias.rearrange("e (q c r) -> q e c r", q=Q, c=HC)[q]).then_inc(s_bias, 16)
            sp.dma_start(bias_down_rows[:, :], down0_b[:, :]).then_inc(s_bias, 16)
            sp.dma_start(raw_view(0, UP), shared_rows[UP][:, :, 0:HALF]).then_inc(s_raw[0][UP], 16)
            sp.dma_start(raw_view(0, DOWN), shared_rows[DOWN][:, 0:IC, :]).then_inc(s_raw[0][DOWN], 16)
            for kind in (GATE, UP):
                sp.dma_start(raw_view(1, kind), shared_rows[kind][:, :, HALF:I]).then_inc(s_raw[1][kind], 16)
            sp.dma_start(raw_view(1, DOWN), shared_rows[DOWN][:, IC:2 * IC, :]).then_inc(s_raw[1][DOWN], 16)
            e_next = pick(1, 0)
            sp.wait_ge(s_tr, batch(0, X_BATCH) + 1)
            load_x(1)
            sp.wait_ge(s_w_lo, 1)
            load_piece(0, e_a)
            for kind, last in ((UP, UP_BATCH + 1), (GATE, GATE_BATCH + 1)):
                sp.wait_ge(s_tr, batch(0, last) + 1)
                load_layer0(kind, e_next)
            for m in (1, 2):
                sp.wait_ge(s_w_lo, m + 1)
                load_piece(m, e_a)
            sp.wait_ge(s_tr, batch(0, DOWN_BATCH + 1) + 1)
            load_layer0(DOWN, e_next)
            for m in range(3, 6):
                sp.wait_ge(s_w_lo, m + 1)
                load_piece(m, e_a)
            e_b = pick(0, 1)
            for m in (6, 7):
                sp.wait_ge(s_w_lo, piece(0, m - 6) + 1)
                load_piece(m, e_b)

            def store(b):
                sp.wait_ge(s_free[0], b + 2)
                sp.wait_ge(s_free[1], b + 2)
                sp.dma_start(out_rows[bass.ds(b, 1)].rearrange("o p c d -> (o p) c d"), y[:, :, :]).then_inc(s_out, 16)

            def rest_of_b(b):
                e = pick(b, 1)
                for m in range(8, PIECES):
                    sp.wait_ge(s_w_lo, piece(b, m - 6) + 1)
                    load_piece(m, e)

            def sample(b, layer0):
                rest_of_b(b)
                if layer0:
                    e0 = pick(b + 2, 0)
                    sp.wait_ge(s_tr, batch(b + 1, X_BATCH) + 1)
                    load_x(b + 2)
                    sp.wait_ge(s_tr, batch(b + 1, UP_BATCH + 1) + 1)
                    load_layer0(UP, e0)
                    sp.wait_ge(s_tr, batch(b + 1, GATE_BATCH + 1) + 1)
                    load_layer0(GATE, e0)
                    sp.wait_ge(s_tr, batch(b + 1, DOWN_BATCH + 1) + 1)
                    load_layer0(DOWN, e0)
                e_first = pick(b + 1, 0)
                for m in range(6):
                    sp.wait_ge(s_w_lo, piece(b, m + 6) + 1)
                    load_piece(m, e_first)
                e_second = pick(b + 1, 1)
                sp.wait_ge(s_w_lo, piece(b + 1, 0) + 1)
                load_piece(6, e_second)
                store(b)
                sp.wait_ge(s_w_lo, piece(b + 1, AHEAD) + 1)
                load_piece(7, e_second)

            with loop(sp, B - 2) as b:
                sample(b, True)
            sample(B - 2, False)
            rest_of_b(B - 1)
            store(B - 1)
            sp.wait_ge(s_out, 16 * (B + 1))

        @block.gpsimd
        def _(pool):
            pool.sem_inc(s_out, 16)
            nc.gpsimd.memset(ident[:, :], 0.0).then_inc(s_ident0, 1)
            nc.gpsimd.memset(ones[:, :], 1.0).then_inc(s_ident, 1)
            pool.wait_ge(s_ident0, 1)
            nc.gpsimd.affine_select(out=ident[:, :], in_=ident[:, :], compare_op=ALU.not_equal, fill=1.0,
                                    base=0, pattern=[[-1, P]], channel_multiplier=1).then_inc(s_ident, 1)

        @block.scalar
        def _(act):
            def split_hi(b, m, place, nth):
                h, kind = m // 3 % 4, m % 3
                act.wait_ge(s_raw[h % 2][kind], 16 * nth)
                nc.scalar.activation(split_view(w_hi[place][kind], kind), raw_order(raw[h % 2][kind], kind),
                                     ACT.Copy).then_inc(s_w_hi, 1)

            def split_hi_shared(m):
                split_hi(0, m, 2 + m // 3, 1)

            def split_hi_routed(b, m):
                if m >= PIECES:
                    b, m = b + 1, m - PIECES
                split_hi(b, m, m // 3 % 2, 2 * b + m // 6 + 2)

            def transposed_hi(s, i):
                act.wait_ge(s_tr, batch(s, i) + 1)
                turned_cols, hi, _ = batch_views(i)
                nc.scalar.activation(hi, turned_cols, ACT.Copy).then_inc(s_tr_hi, 1)

            def activate(n, r, kind, k, e):
                act.wait_ge(s_gu, n + 1)
                if kind == "L":
                    for c in range(2):
                        ins = nc.scalar.activation(act_out[:, r, c, :], up_ps[r][:, c, :], ACT.Silu,
                                                   bias=bias_up[:, bass.ds(e * HC + 2 * k + c, 1)])
                    ins.then_inc(s_act, 1)
                else:
                    nc.scalar.activation(act_out[:, r, :, :].rearrange("p a b -> p (a b)"),
                                         gate_ps[r][:, :, :].rearrange("p a b -> p (a b)"),
                                         ACT.Gelu_apprx_tanh).then_inc(s_act, 1)

            def hidden_hi(n, r, used=True):
                act.wait_ge(s_mul, n + 1)
                if used:
                    act.wait_ge(s_down, n - 1)
                nc.scalar.activation(h_hi[r][:, :, :].rearrange("p a b -> p (a b)"),
                                     hidden[:, r, :, :].rearrange("p a b -> p (a b)"), ACT.Copy).then_inc(s_h_hi, 1)

            def last_activate(n, r):
                act.wait_ge(s_gu, n + 1)
                for c, done in enumerate((s_act_c0, s_act)):
                    nc.scalar.activation(act_out[:, r, c, :], gate_ps[r][:, c, :],
                                         ACT.Gelu_apprx_tanh).then_inc(done, 1)

            def last_hidden_hi(n, r, b):
                act.wait_ge(s_down, n - 1)
                act.wait_ge(s_mul_c0, b + 1)
                nc.scalar.activation(h_hi[r][:, 0, :], hidden[:, r, 0, :], ACT.Copy).then_inc(s_h_hi_c0, 1)
                act.wait_ge(s_mul, n + 1)
                nc.scalar.activation(h_hi[r][:, 1, :], hidden[:, r, 1, :], ACT.Copy).then_inc(s_h_hi, 1)

            def next_x1_hi(s):
                act.wait_ge(s_x1T, s + 1)
                nc.scalar.activation(x1_hi[:, :, :].rearrange("p a b -> p (a b)"),
                                     x1T[:, :, :].rearrange("p a b -> p (a b)"), ACT.Copy).then_inc(s_x1_hi, 1)

            def evacuate(b, n_last):
                act.wait_ge(s_down, n_last + 1)
                act.wait_ge(s_out, 16 * (b + 1))
                nc.scalar.activation(y_cols(0), sum_cols(0), ACT.Copy).then_inc(s_free[0], 1)

            def pick(s):
                return act.value_load(expert[0:1, bass.ds(s, 1), 0:1].rearrange("p a b -> p (a b)"),
                                      min_val=0, max_val=E - 1)

            act.wait_ge(s_top, 1)
            nc.scalar.activation(exps[:, :], top[:, :], ACT.Exp, bias=neg_max[:, 0:1],
                                 accum_out=exp_sum[:, 0:1]).then_inc(s_exp, 1)

            transposed_hi(0, X_BATCH)
            split_hi_shared(0)
            act.wait_ge(s_expert, 1)
            e0 = pick(0)
            for i in range(1, BATCHES):
                transposed_hi(0, i)
            nc.scalar.preload_act_table(ACT.Silu)
            split_hi_shared(1)
            act.wait_ge(s_free[1], 1)
            for k in range(2):
                activate(k, k, "L", k, e0)
                hidden_hi(k, k, used=False)
            for m in (2, 3):
                split_hi_shared(m)
            next_x1_hi(0)
            for m in (4, 5):
                split_hi_shared(m)
            split_hi_routed(0, 0)

            nc.scalar.preload_act_table(ACT.Gelu_apprx_tanh)
            with loop(act, B - 1) as b:
                e0 = pick(b + 1)
                split_hi_routed(b, AHEAD)
                for j, (kind, k) in enumerate(PLAN[:-1]):
                    n = position(b, j)
                    activate(n, j % 2, kind, k, e0)
                    hidden_hi(n, j % 2)
                    if j in BATCH_AT:
                        transposed_hi(b + 1, BATCH_AT[j])
                    for m in SPLIT_AT.get(j, ()):
                        split_hi_routed(b, m)
                n, r = position(b, NPOS - 1), (NPOS - 1) % 2
                last_activate(n, r)
                next_x1_hi(b + 1)
                last_hidden_hi(n, r, b)
                evacuate(b, n)
            b = B - 1
            split_hi_routed(b, AHEAD)
            for j, (kind, k) in enumerate(LAST_PLAN[:-1]):
                n = position(b, j)
                activate(n, j % 2, kind, k, None)
                hidden_hi(n, j % 2)
                for m in LAST_SPLIT_AT.get(j, ()):
                    split_hi_routed(b, m)
            n, r = position(b, len(LAST_PLAN) - 1), (len(LAST_PLAN) - 1) % 2
            last_activate(n, r)
            last_hidden_hi(n, r, b)
            evacuate(b, n)

        @block.vector
        def _(dve):
            def split_lo(m, place, number):
                h, kind = m // 3 % 4, m % 3
                dve.wait_ge(s_w_hi, number + 1)
                nc.vector.tensor_tensor(split_view(w_lo[place][kind], kind), raw_order(raw[h % 2][kind], kind),
                                        split_view(w_hi[place][kind], kind).bitcast(F32),
                                        ALU.subtract).then_inc(s_w_lo, 1)

            def split_lo_shared(m):
                split_lo(m, 2 + m // 3, m)

            def split_lo_routed(b, m):
                if m >= PIECES:
                    b, m = b + 1, m - PIECES
                split_lo(m, m // 3 % 2, piece(b, m))

            def transpose_batch(s, i):
                if i >= 3:
                    dve.wait_ge(s_tr_lo, batch(s, i - 2) + 1)
                if i == X_BATCH:
                    dve.wait_ge(s_x, 16 * Q * (s + 1))
                    dst = xT[:, :, :].rearrange("p c (n r) -> p c n r", r=BLK)
                    src = x_raw[:, :, :].rearrange("p n (a c) -> p c n a", c=DC)
                elif i < DOWN_BATCH:
                    kind, dc = (UP, i - UP_BATCH) if i < GATE_BATCH else (GATE, i - GATE_BATCH)
                    dve.wait_ge(s_w0[kind], 16 * Q * (s + 1))
                    raw0 = up0_raw if kind == UP else gate0_raw
                    dst = turned[i % 2][:, :].rearrange("p (c q r) -> p q c r", c=HC, q=Q)
                    src = raw0[:, :, :].rearrange("p (q c) (a k) -> p k q c a", q=Q, k=DC)[:, dc]
                else:
                    dve.wait_ge(s_w0[DOWN], 16 * Q * (s + 1))
                    k = 2 * (i - DOWN_BATCH)
                    dst = turned[i % 2][:, :].rearrange("p (c n r) -> p c n r", c=2, r=BLK)
                    src = down0_raw[:, :, k * BLK:(k + 2) * BLK].rearrange("p n (c a) -> p c n a", c=2)
                nc.vector.transpose(dst, src).then_inc(s_tr, 1)

            def transposed_lo(s, i):
                dve.wait_ge(s_tr_hi, batch(s, i) + 1)
                turned_cols, hi, lo = batch_views(i)
                nc.vector.tensor_tensor(lo, turned_cols, hi.bitcast(F32), ALU.subtract).then_inc(s_tr_lo, 1)

            def multiply(n, r, kind, k, b, e):
                dve.wait_ge(s_act, n + 1)
                flat = "p a b -> p (a b)"
                if kind == "L":
                    for c in range(2):
                        ins = nc.vector.scalar_tensor_tensor(
                            out=hidden[:, r, c, :], in0=gate_ps[r][:, c, :],
                            scalar=bias_gate[:, bass.ds(e * HC + 2 * k + c, 1)], in1=act_out[:, r, c, :],
                            op0=ALU.add, op1=ALU.mult)
                    ins.then_inc(s_mul, 1)
                elif kind == "S":
                    nc.vector.tensor_tensor(hidden[:, r, :, :].rearrange(flat), up_ps[r][:, :, :].rearrange(flat),
                                            act_out[:, r, :, :].rearrange(flat), ALU.mult).then_inc(s_mul, 1)
                else:
                    nc.vector.scalar_tensor_tensor(
                        out=hidden[:, r, :, :].rearrange(flat), in0=act_out[:, r, :, :].rearrange(flat),
                        scalar=route[:, bass.ds(b, 1), "AB".index(kind):"AB".index(kind) + 1].rearrange(flat),
                        in1=up_ps[r][:, :, :].rearrange(flat), op0=ALU.mult, op1=ALU.mult).then_inc(s_mul, 1)

            def hidden_lo(n, r):
                dve.wait_ge(s_h_hi, n + 1)
                flat = "p a b -> p (a b)"
                nc.vector.tensor_tensor(h_lo[r][:, :, :].rearrange(flat), hidden[:, r, :, :].rearrange(flat),
                                        h_hi[r][:, :, :].rearrange(flat).bitcast(F32), ALU.subtract).then_inc(s_h_lo, 1)

            def last_multiply(n, r, b):
                for c, (ready, value, done) in enumerate(((s_act_c0, b + 1, s_mul_c0), (s_act, n + 1, s_mul))):
                    dve.wait_ge(ready, value)
                    nc.vector.scalar_tensor_tensor(
                        out=hidden[:, r, c, :], in0=act_out[:, r, c, :],
                        scalar=route[:, bass.ds(b, 1), 1:2].rearrange("p a b -> p (a b)"),
                        in1=up_ps[r][:, c, :], op0=ALU.mult, op1=ALU.mult).then_inc(done, 1)

            def last_hidden_lo(n, r, b):
                for c, (ready, value, done) in enumerate(((s_h_hi_c0, b + 1, s_h_lo_c0), (s_h_hi, n + 1, s_h_lo))):
                    dve.wait_ge(ready, value)
                    nc.vector.tensor_tensor(h_lo[r][:, c, :], hidden[:, r, c, :], h_hi[r][:, c, :].bitcast(F32),
                                            ALU.subtract).then_inc(done, 1)

            def next_x1T(s, n, e):
                dve.wait_ge(s_down, n + 1)
                for dc in range(DC):
                    ins = nc.vector.scalar_tensor_tensor(
                        out=x1T[:, dc, :], in0=sum0_ps[dc][:, 0:S],
                        scalar=bias_down[:, bass.ds(e + dc * E, 1)],
                        in1=xT[:, dc, :], op0=ALU.add, op1=ALU.add)
                ins.then_inc(s_x1T, 1)

            def next_x1_lo(s):
                dve.wait_ge(s_x1_hi, s + 1)
                flat = "p a b -> p (a b)"
                nc.vector.tensor_tensor(x1_lo[:, :, :].rearrange(flat), x1T[:, :, :].rearrange(flat),
                                        x1_hi[:, :, :].rearrange(flat).bitcast(F32), ALU.subtract).then_inc(s_x1_lo, 1)

            def evacuate(b, n_last):
                dve.wait_ge(s_down, n_last + 1)
                dve.wait_ge(s_out, 16 * (b + 1))
                nc.vector.tensor_copy(y_cols(1), sum_cols(1)).then_inc(s_free[1], 1)

            def pick(s):
                return dve.value_load(expert[0:1, bass.ds(s, 1), 0:1].rearrange("p a b -> p (a b)"),
                                      min_val=0, max_val=E - 1)

            links = [0]

            def chained(ins):
                links[0] += 1
                ins.then_inc(s_chain, 1)
                dve.wait_ge(s_chain, links[0])

            dve.wait_ge(s_cond, 16)
            chained(nc.vector.max(top[:, :], logits[:, :]))
            nc.vector.tensor_scalar(neg_max[:, :], top[:, 0:1], -1.0, None, ALU.mult).then_inc(s_top, 1)
            chained(nc.vector.max_index(top_at[:, :], top[:, :], logits[:, :]))
            chained(nc.vector.tensor_copy(choice[:, :], top_at[:, 0:2]))

            def diagonal(dst, src):
                return nc.vector.tensor_tensor(dst[:, :, :],
                                               src[:, :].rearrange("p (o c) -> p o c", o=1).to_broadcast([B, B, 2]),
                                               ident[0:B, 0:B].rearrange("p (b o) -> p b o", o=1).to_broadcast([B, B, 2]),
                                               ALU.mult)

            dve.wait_ge(s_ident, 2)
            diagonal(choice_diag, choice).then_inc(s_diag, 1)
            dve.wait_ge(s_exp, 1)
            chained(nc.vector.reciprocal(exp_inv[:, :], exp_sum[:, :]))
            dve.wait_ge(s_spread, 1)
            nc.vector.tensor_copy(expert[:, :, :].rearrange("p b c -> p (b c)"), sum0_ps[1][:, 0:2 * B]).then_inc(s_expert, 1)
            chained(nc.vector.tensor_scalar(probs[:, :], exps[:, 0:2], exp_inv[:, 0:1], None, ALU.mult))
            chained(nc.vector.tensor_tensor(pair_sum[:, :], probs[:, 0:1], probs[:, 1:2], ALU.add))
            chained(nc.vector.reciprocal(pair_inv[:, :], pair_sum[:, :]))
            chained(nc.vector.tensor_scalar(pair_w[:, :], probs[:, :], pair_inv[:, 0:1], None, ALU.mult))
            chained(nc.vector.tensor_scalar(pair_w2[:, :], pair_w[:, :], 1.0 - MIX, None, ALU.mult))
            chained(nc.vector.scalar_tensor_tensor(out=weight[:, :], in0=pair_w[:, :], scalar=MIX, in1=pair_w2[:, :],
                                                   op0=ALU.mult, op1=ALU.add))
            diagonal(weight_diag, weight).then_inc(s_wdiag, 1)
            dve.wait_ge(s_wspread, 1)
            nc.vector.tensor_copy(route[:, :, :].rearrange("p b c -> p (b c)"), out_ps[0][:, 0:2 * B]).then_inc(s_free[0], 1)

            dve.wait_ge(s_expert, 1)
            e0 = pick(0)
            transpose_batch(0, X_BATCH)
            transposed_lo(0, X_BATCH)
            split_lo_shared(0)
            transpose_batch(0, 1)
            for i in range(1, BATCHES):
                if i + 1 < BATCHES:
                    transpose_batch(0, i + 1)
                transposed_lo(0, i)
            dve.wait_ge(s_biasT, 1)
            nc.vector.tensor_copy(bias_up[:, :], out_ps[1][:, 0:E * HC])
            nc.vector.tensor_copy(bias_gate[:, :], out_ps[1][:, P:P + E * HC])
            nc.vector.tensor_copy(bias_down[:, :], out_ps[1][:, 2 * P:2 * P + E * DC]).then_inc(s_free[1], 1)
            split_lo_shared(1)
            dve.wait_ge(s_free[1], 1)
            for k in range(2):
                multiply(k, k, "L", k, None, e0)
                hidden_lo(k, k)
            for m in (2, 3):
                split_lo_shared(m)
            next_x1T(0, 1, e0)
            next_x1_lo(0)
            for m in (4, 5):
                split_lo_shared(m)
            dve.wait_ge(s_free[0], 1)
            split_lo_routed(0, 0)

            x1_at = PLAN.index(("L", 1)) + LAG + 1
            with loop(dve, B - 1) as b:
                e0 = pick(b + 1)
                split_lo_routed(b, AHEAD)
                for j, (kind, k) in enumerate(PLAN[:-1]):
                    n = position(b, j)
                    if j == x1_at:
                        next_x1T(b + 1, position(b, j - LAG - 1), e0)
                    multiply(n, j % 2, kind, k, b, e0)
                    if j in BATCH_AT:
                        transpose_batch(b + 1, BATCH_AT[j])
                    for m in SPLIT_AT.get(j - 1, ()):
                        split_lo_routed(b, m)
                    hidden_lo(n, j % 2)
                    if j in BATCH_AT:
                        transposed_lo(b + 1, BATCH_AT[j])
                n, r = position(b, NPOS - 1), (NPOS - 1) % 2
                last_multiply(n, r, b)
                last_hidden_lo(n, r, b)
                next_x1_lo(b + 1)
                evacuate(b, n)
            b = B - 1
            split_lo_routed(b, AHEAD)
            for j, (kind, k) in enumerate(LAST_PLAN[:-1]):
                n = position(b, j)
                multiply(n, j % 2, kind, k, b, None)
                for m in LAST_SPLIT_AT.get(j - 1, ()):
                    split_lo_routed(b, m)
                hidden_lo(n, j % 2)
            n, r = position(b, len(LAST_PLAN) - 1), (len(LAST_PLAN) - 1) % 2
            last_multiply(n, r, b)
            last_hidden_lo(n, r, b)
            evacuate(b, n)

        @block.tensor
        def _(pe):
            def three_passes(ps, w, m, first, last):
                nc.tensor.matmul(ps, w[0], m[0], start=first, stop=False)
                nc.tensor.matmul(ps, w[0], m[1], start=False, stop=False)
                return nc.tensor.matmul(ps, w[1], m[0], start=False, stop=last)

            def gate_up(n, r, kind, k, fresh=False):
                if not fresh:
                    pe.wait_ge(s_mul, n - 1)
                for c in range(2):
                    for ps, what in ((gate_ps, GATE), (up_ps, UP)):
                        for dc in range(DC):
                            if kind == "L":
                                col = slice((2 * k + c) * P, (2 * k + c + 1) * P)
                                hi, lo = (gate0_hi, gate0_lo) if what == GATE else (up0_hi, up0_lo)
                                w = hi[:, dc, col], lo[:, dc, col]
                                m = xT_hi[:, dc, :], xT_lo[:, dc, :]
                            else:
                                w = chunk(half_of(kind, k), what, dc, 2 * (k % 2) + c)
                                m = x1_hi[:, dc, :], x1_lo[:, dc, :]
                            ins = three_passes(ps[r][:, c, :], w, m, dc == 0, dc == DC - 1)
                ins.then_inc(s_gu, 1)

            def down(n, r, kind, k, first, last, b=None):
                if not last:
                    pe.wait_ge(s_h_lo, n + 1)
                if kind == "L":
                    for c in range(2):
                        hc = 2 * k + c
                        for dc in range(DC):
                            col = slice(dc * P, (dc + 1) * P)
                            ins = three_passes(sum0_ps[dc][:, 0:S],
                                               (down0_hi[:, hc, col], down0_lo[:, hc, col]),
                                               (h_hi[r][:, c, :], h_lo[r][:, c, :]),
                                               hc == 0, hc == HC - 1)
                else:
                    if first:
                        for sc in range(SC):
                            for dc in range(DC):
                                nc.tensor.matmul(out_ps[sc][:, dc * P:(dc + 1) * P], x1T[:, dc, sc * P:(sc + 1) * P],
                                                 ident[:, :], is_transpose=True, start=(dc == 0), stop=False,
                                                 skip_group_check=True)
                    place = half_of(kind, k)
                    for c in range(2):
                        if last:
                            pe.wait_ge(*((s_h_lo_c0, b + 1) if c == 0 else (s_h_lo, n + 1)))
                        at = (2 * (k % 2) + c) * D
                        w = w_hi[place][DOWN][:, at:at + D], w_lo[place][DOWN][:, at:at + D]
                        for sc in range(SC):
                            col = slice(sc * P, (sc + 1) * P)
                            h = h_hi[r][:, c, col], h_lo[r][:, c, col]
                            ps = out_ps[sc][:, 0:D]
                            for a, (i1, i2) in enumerate(((0, 0), (0, 1), (1, 0))):
                                ins = nc.tensor.matmul(ps, h[i1], w[i2], start=False,
                                                       stop=(last and c == 1 and a == 2), skip_group_check=True)
                ins.then_inc(s_down, 1)

            pe.wait_ge(s_ident, 2)
            pe.wait_ge(s_diag, 1)
            nc.tensor.matmul(sum0_ps[1][:, 0:2 * B], ones[:, :], choice_diag[:, :, :].rearrange("p a b -> p (a b)"),
                             start=True, stop=True).then_inc(s_spread, 1)
            pe.wait_ge(s_wdiag, 1)
            nc.tensor.matmul(out_ps[0][:, 0:2 * B], ones[:, :], weight_diag[:, :, :].rearrange("p a b -> p (a b)"),
                             start=True, stop=True).then_inc(s_wspread, 1)
            pe.wait_ge(s_bias, 16 * (2 * Q + 1))
            for c in range(2):
                nc.tensor.transpose(out_ps[1][:, c * P:c * P + E * HC], bias_rows[:, c, :], ident[0:E * HC, 0:E * HC])
            for dc in range(DC):
                at = 2 * P + dc * E
                ins = nc.tensor.transpose(out_ps[1][:, at:at + E],
                                          bias_down_rows[:, :].rearrange("e (p c) -> e c p", c=DC)[:, dc, :],
                                          ident[0:E, 0:E])
            ins.then_inc(s_biasT, 1)
            pe.wait_ge(s_tr_lo, batch(0, GATE_BATCH + 1) + 1)
            for k in range(2):
                gate_up(k, k, "L", k, fresh=True)
            pe.wait_ge(s_tr_lo, batch(0, DOWN_BATCH + 1) + 1)
            pe.wait_ge(s_expert, 1)
            for k in range(2):
                down(k, k, "L", k, False, False)
            pe.wait_ge(s_w_lo, 2)

            def sample(b, plan, layer0):
                steps = len(plan)
                pe.wait_ge(s_x1_lo, b + 1)
                for j in range(steps + LAG):
                    if j < steps:
                        kind, k = plan[j]
                        if kind in "AB" and k % 2 == 0:
                            pe.wait_ge(s_w_lo, piece(b, 6 * (kind == "B") + 3 * (k // 2) + UP) + 1)
                        if kind == "L" and k == 0:
                            pe.wait_ge(s_tr_lo, batch(b + 1, GATE_BATCH + 1) + 1)
                        gate_up(position(b, j), j % 2, kind, k)
                    if j >= LAG:
                        kind, k = plan[j - LAG]
                        if kind in "AB" and k % 2 == 0:
                            pe.wait_ge(s_w_lo, piece(b, 6 * (kind == "B") + 3 * (k // 2) + DOWN) + 1)
                        if kind == "L" and k == 0:
                            pe.wait_ge(s_tr_lo, batch(b + 1, DOWN_BATCH + 1) + 1)
                            pe.wait_ge(s_x1T, b + 1)
                        if j == LAG:
                            pe.wait_ge(s_free[0], b + 1)
                            pe.wait_ge(s_free[1], b + 1)
                        down(position(b, j - LAG), j % 2, kind, k, j == LAG, j == steps + LAG - 1, b)

            with loop(pe, B - 1) as b:
                sample(b, PLAN, True)
            sample(B - 1, LAST_PLAN, False)


_INS = ['x', 'cond_8', 'L0_cond_W_up', 'L0_cond_b_up', 'L0_cond_W_gate', 'L0_cond_b_gate', 'L0_cond_W_down',
        'L0_cond_b_down', 'L1_cond_skill_gate', 'L1_cond_skill_up', 'L1_cond_skill_down', 'L1_cond_shared_gate',
        'L1_cond_shared_up', 'L1_cond_shared_down']


def kernel(**inputs):
    import numpy as _np
    import concourse.bacc as _bacc
    from concourse import mybir as _mybir
    from concourse.bass_utils import run_bass_kernel_spmd as _run

    nc = _bacc.Bacc("TRN2", target_bir_lowering=False, num_devices=1)
    arrays, args = {}, []
    for name in _INS:
        a = _np.ascontiguousarray(inputs[name])
        arrays[f"in_{name}_dram"] = a
        args.append(nc.dram_tensor(f"in_{name}_dram", a.shape, _mybir.dt.from_np(a.dtype), kind="ExternalInput").ap())
    shape = arrays["in_x_dram"].shape
    args.append(nc.dram_tensor("out_dram", shape, _mybir.dt.float32, kind="ExternalOutput").ap())
    bass_cond_two_layer_kernel(nc, *args)
    r = _run(nc, [arrays], core_ids=[0])
    return r.results[0]["out_dram"]
```

```python
from contextlib import ExitStack

import concourse.bass as bass
from concourse import mybir

P = 128
ALU = mybir.AluOpType
ACT = mybir.ActivationFunctionType
F32 = mybir.dt.float32
F32R = mybir.dt.float32r
I32 = mybir.dt.int32
U32 = mybir.dt.uint32

NUM_MOE_LAYERS = 12
MIX = 1.0 / NUM_MOE_LAYERS

PLAN = [("S", 0), ("S", 1), ("A", 0), ("A", 1), ("S", 2), ("A", 2), ("A", 3),
        ("L", 0), ("L", 1), ("B", 0), ("B", 1), ("S", 3), ("B", 2), ("B", 3)]
LAST_PLAN = [step for step in PLAN if step[0] != "L"]
NPOS = len(PLAN)
LAG = 2

GATE, UP, DOWN = range(3)
PIECES = 12
SPLIT_AT = {0: [2], 1: [3], 2: [4], 3: [5], 5: [6], 6: [7], 7: [8], 8: [9], 9: [10], 10: [11], 11: [12]}
LAST_SPLIT_AT = {0: [2], 1: [3], 2: [4, 5], 3: [6], 4: [7], 5: [8], 6: [9], 7: [10], 8: [11]}
AHEAD = 1
KEEP_AT = 4
SHARED_PIECES = 6

WARM_LOADS, WARM_HIDDEN, WARM_X1 = 12, 6, 8

BLK = 32
X_BATCH, UP_BATCH, GATE_BATCH, DOWN_BATCH = 0, 1, 3, 5
BATCHES = 7
BATCH_AT = {0: 0, 1: 1, 2: 2, 3: 3, 4: 4, 6: 5, 7: 6}


def bass_cond_two_layer_kernel(
    nc: bass.Bass,
    x: bass.AP,
    cond: bass.AP,
    up0_w: bass.AP,
    up0_b: bass.AP,
    gate0_w: bass.AP,
    gate0_b: bass.AP,
    down0_w: bass.AP,
    down0_b: bass.AP,
    skill_gate: bass.AP,
    skill_up: bass.AP,
    skill_down: bass.AP,
    shared_gate: bass.AP,
    shared_up: bass.AP,
    shared_down: bass.AP,
    out: bass.AP,
):
    B, S, D = x.shape
    E, H = up0_b.shape
    I = shared_gate.shape[1]
    DC, HC = D // P, H // P
    HALF = I // 2
    IC = HALF // P
    assert (S, DC, HC, IC) == (2 * P, 2, 4, 4) and cond.shape == (B, E) and E == 8
    Q = P // BLK
    DQ, HQ = D // Q, H // Q

    def position(b, j):
        return 2 + NPOS * b + j

    def piece(b, m):
        return PIECES * b + m

    def batch(s, i):
        return BATCHES * s + i

    ctx = ExitStack()
    with ctx:
        def sb(name, shape, dt=F32):
            return ctx.enter_context(nc.sbuf_tensor(name, shape, dt))

        def bank(name, shape):
            return ctx.enter_context(nc.psum_tensor(name, shape, F32))

        def sem(name):
            return ctx.enter_context(nc.semaphore(name))

        ident = sb("ident", [P, P])
        ones = sb("ones", [B, P])
        logits = sb("logits", [B, E])
        top = sb("top", [B, 8])
        top_at = sb("top_at", [B, 8], U32)
        neg_max = sb("neg_max", [B, 1])
        exps = sb("exps", [B, 8])
        exp_sum = sb("exp_sum", [B, 1])
        exp_inv = sb("exp_inv", [B, 1])
        probs = sb("probs", [B, 2])
        pair_sum = sb("pair_sum", [B, 1])
        pair_inv = sb("pair_inv", [B, 1])
        pair_w = sb("pair_w", [B, 2])
        pair_w2 = sb("pair_w2", [B, 2])
        choice = sb("choice", [B, 2])
        choice_diag = sb("choice_diag", [B, B, 2])
        weight = sb("weight", [B, 2])
        weight_diag = sb("weight_diag", [B, B, 2])
        route = sb("route", [P, B, 2])
        expert = sb("expert", [P, B, 2], I32)
        bias_rows = sb("bias_rows", [E * HC, 2, P])
        bias_down_rows = sb("bias_down_rows", [E, D])
        bias_up = sb("bias_up", [P, E * HC])
        bias_gate = sb("bias_gate", [P, E * HC])
        bias_down = sb("bias_down", [P, E * DC])

        x_raw = sb("x_raw", [P, S // BLK, DQ])
        up0_raw = sb("up0_raw", [P, H // BLK, DQ])
        gate0_raw = sb("gate0_raw", [P, H // BLK, DQ])
        down0_raw = sb("down0_raw", [P, D // BLK, HQ])
        turned = [sb(f"turned{r}", [P, H]) for r in range(2)]
        xT = sb("xT", [P, DC, S])
        xT_hi, xT_lo = sb("xT_hi", [P, DC, S], F32R), sb("xT_lo", [P, DC, S], F32R)
        up0_hi, up0_lo = sb("up0_hi", [P, DC, H], F32R), sb("up0_lo", [P, DC, H], F32R)
        gate0_hi, gate0_lo = sb("gate0_hi", [P, DC, H], F32R), sb("gate0_lo", [P, DC, H], F32R)
        down0_hi, down0_lo = sb("down0_hi", [P, HC, D], F32R), sb("down0_lo", [P, HC, D], F32R)

        x1T = sb("x1T", [P, DC, S])
        x1_hi, x1_lo = sb("x1_hi", [P, DC, S], F32R), sb("x1_lo", [P, DC, S], F32R)
        raw = [[sb(f"raw{r}_{k}", [P, DC * HALF]) for k in ("gate", "up", "down")] for r in range(2)]
        w_hi = [[sb(f"w_hi{r}_{k}", [P, DC * HALF], F32R) for k in ("gate", "up", "down")] for r in range(4)]
        w_lo = [[sb(f"w_lo{r}_{k}", [P, DC * HALF], F32R) for k in ("gate", "up", "down")] for r in range(4)]

        act_out = sb("act_out", [P, 2, 2, S])
        hidden = sb("hidden", [P, 2, 2, S])
        h_hi = [sb(f"h_hi{r}", [P, 2, S], F32R) for r in range(2)]
        h_lo = [sb(f"h_lo{r}", [P, 2, S], F32R) for r in range(2)]
        total = sb("total", [P, DC, S])
        y = sb("y", [P, S // BLK, DQ])

        gate_ps = [bank(f"gate_ps{r}", [P, 2, S]) for r in range(2)]
        up_ps = [bank(f"up_ps{r}", [P, 2, S]) for r in range(2)]
        sum0_ps = [bank(f"sum0_ps{r}", [P, 512]) for r in range(2)]
        out_ps = [bank(f"out_ps{r}", [P, 512]) for r in range(2)]

        s_ident0 = sem("ident_zeroed")
        s_ident = sem("ident_ready")
        s_cond = sem("cond_loaded")
        s_bias_up = sem("bias_up_loaded")
        s_bias = sem("bias_gate_and_down_loaded")
        s_chain = sem("vector_chain")
        s_top = sem("top_ready")
        s_exp = sem("exps_ready")
        s_top_at = sem("top_at_ready")
        s_diag = sem("choice_diag_ready")
        s_spread = sem("choices_spread")
        s_wdiag = sem("weight_diag_ready")
        s_wspread = sem("weights_spread")
        s_expert = sem("experts_ready")
        s_biasT = sem("bias_transposed")
        s_bias_up_cols = sem("bias_up_columns_ready")
        s_x = sem("x_loaded")
        s_w0 = [sem(f"layer0_{k}_loaded") for k in ("gate", "up", "down")]
        s_raw = [[sem(f"raw{r}_{k}_loaded") for k in ("gate", "up", "down")] for r in range(2)]
        s_tr = sem("batch_transposed")
        s_tr_hi = sem("batch_hi_ready")
        s_tr_lo = sem("batch_lo_ready")
        s_shared_hi = sem("shared_piece_hi_ready")
        s_shared_lo = sem("shared_piece_lo_ready")
        s_w_hi = sem("piece_hi_ready")
        s_w_lo = sem("piece_lo_ready")
        s_up0 = sem("first_layer0_up_done")
        s_gu = sem("gate_up_done")
        s_act = sem("act_done")
        s_mul = sem("hidden_done")
        s_h_hi = sem("hidden_hi_ready")
        s_h_lo = sem("hidden_lo_ready")
        s_down = sem("down_done")
        s_act_c0 = sem("last_act_chunk0_done")
        s_mul_c0 = sem("last_hidden_chunk0_done")
        s_h_hi_c0 = sem("last_hidden_chunk0_hi_ready")
        s_h_lo_c0 = sem("last_hidden_chunk0_lo_ready")
        s_x1T = sem("x1T_ready")
        s_x1_hi = sem("x1_hi_ready")
        s_x1_lo = sem("x1_lo_ready")
        s_route = sem("route_ready")
        s_free = sem("out_banks_read")
        s_res = sem("residual_kept")
        s_y = sem("y_ready")
        s_out = sem("out_stored")

        def half_of(kind, k):
            return k // 2 + (2 if kind == "S" else 0)

        def chunk(r, kind, dc, ic):
            c = dc * HALF + ic * P
            return w_hi[r][kind][:, c:c + P], w_lo[r][kind][:, c:c + P]

        def raw_order(t, kind):
            return t[:, :].rearrange("p (k a c) -> p k c a", c=DC, a=P) if kind == DOWN else t[:, :]

        def split_view(t, kind):
            return t[:, :].rearrange("p (k c a) -> p k c a", c=DC, a=P) if kind == DOWN else t[:, :]

        def batch_views(i):
            flat = "p a b -> p (a b)"
            if i == X_BATCH:
                return tuple(t[:, :, :].rearrange(flat) for t in (xT, xT_hi, xT_lo))
            t = turned[i % 2]
            if i < GATE_BATCH:
                return t[:, :], up0_hi[:, i - UP_BATCH, :], up0_lo[:, i - UP_BATCH, :]
            if i < DOWN_BATCH:
                return t[:, :], gate0_hi[:, i - GATE_BATCH, :], gate0_lo[:, i - GATE_BATCH, :]
            k = 2 * (i - DOWN_BATCH)
            return (t[:, :].rearrange("p (k a c) -> p k c a", c=DC, a=P),
                    down0_hi[:, k:k + 2, :].rearrange("p k (c a) -> p k c a", c=DC),
                    down0_lo[:, k:k + 2, :].rearrange("p k (c a) -> p k c a", c=DC))

        def loop(eng, count):
            return nc.Fori(0, count, engines=(eng.engine,), hint_back_edge=True)

        block = ctx.enter_context(nc.Block())

        @block.sync
        def _(sp):
            x_blocks = x.rearrange("b (n r) (q k) -> b q r n k", r=BLK, q=Q)
            out_blocks = out.rearrange("b (n r) (q k) -> b q r n k", r=BLK, q=Q)
            layer0_blocks = [gate0_w.rearrange("e (n r) (q k) -> e q r n k", r=BLK, q=Q),
                             up0_w.rearrange("e (n r) (q k) -> e q r n k", r=BLK, q=Q),
                             down0_w.rearrange("e (n r) (q k) -> e q r n k", r=BLK, q=Q)]
            layer0_raw = [gate0_raw, up0_raw, down0_raw]
            skill_rows = [skill_gate.rearrange("e (p c) i -> e p c i", p=P),
                          skill_up.rearrange("e (p c) i -> e p c i", p=P),
                          skill_down.rearrange("e (c p) d -> e p c d", p=P)]
            shared_rows = [shared_gate.rearrange("(p c) i -> p c i", p=P),
                           shared_up.rearrange("(p c) i -> p c i", p=P),
                           shared_down.rearrange("(c p) d -> p c d", p=P)]

            def raw_view(r, kind):
                return raw[r][kind][:, :].rearrange("p (c n) -> p c n", c=(IC if kind == DOWN else DC))

            def load_blocks(raw, blocks, at, loaded):
                for q in range(Q):
                    sp.dma_start(raw[q * BLK:(q + 1) * BLK, :, :],
                                 blocks[bass.ds(at, 1), q].rearrange("o r n k -> (o r) n k")).then_inc(loaded, 16)

            def load_x(s):
                load_blocks(x_raw, x_blocks, s, s_x)

            def load_layer0(kind, e):
                load_blocks(layer0_raw[kind], layer0_blocks[kind], e, s_w0[kind])

            def load_piece(m, e):
                h, kind = m // 3, m % 3
                k = h % 2
                rows = skill_rows[kind][bass.ds(e, 1)].rearrange("o p c n -> (o p) c n")
                part = rows[:, k * IC:(k + 1) * IC, :] if kind == DOWN else rows[:, :, k * HALF:(k + 1) * HALF]
                sp.dma_start(raw_view(h % 2, kind), part).then_inc(s_raw[h % 2][kind], 16)

            def pick(s, choice_no):
                return sp.value_load(expert[0:1, bass.ds(s, 1), choice_no:choice_no + 1].rearrange("p a b -> p (a b)"),
                                     min_val=0, max_val=E - 1)

            sp.dma_start(logits[:, :], cond[:, :]).then_inc(s_cond, 16)
            load_x(0)
            sp.wait_ge(s_top_at, 1)
            e_a = sp.value_load(top_at[0:1, 0:1], min_val=0, max_val=E - 1)
            for kind in (UP, GATE, DOWN):
                load_layer0(kind, e_a)
            sp.dma_start(raw_view(0, GATE), shared_rows[GATE][:, :, 0:HALF]).then_inc(s_raw[0][GATE], 16)
            sp.dma_start(raw_view(0, UP), shared_rows[UP][:, :, 0:HALF]).then_inc(s_raw[0][UP], 16)
            sp.dma_start(raw_view(0, DOWN), shared_rows[DOWN][:, 0:IC, :]).then_inc(s_raw[0][DOWN], 16)
            for kind in (GATE, UP):
                sp.dma_start(raw_view(1, kind), shared_rows[kind][:, :, HALF:I]).then_inc(s_raw[1][kind], 16)
            sp.dma_start(raw_view(1, DOWN), shared_rows[DOWN][:, IC:2 * IC, :]).then_inc(s_raw[1][DOWN], 16)
            sp.wait_ge(s_expert, 1)
            e_next = pick(1, 0)
            sp.wait_ge(s_tr, batch(0, X_BATCH) + 1)
            load_x(1)
            for m in (0, 1):
                sp.wait_ge(s_shared_lo, m + 1)
                load_piece(m, e_a)
            sp.wait_ge(s_tr, batch(0, UP_BATCH + 1) + 1)
            load_layer0(UP, e_next)
            for m in (2, 3, 4):
                sp.wait_ge(s_shared_lo, m + 1)
                load_piece(m, e_a)
            sp.wait_ge(s_tr, batch(0, GATE_BATCH + 1) + 1)
            load_layer0(GATE, e_next)
            sp.wait_ge(s_shared_lo, 6)
            load_piece(5, e_a)
            sp.wait_ge(s_tr, batch(0, DOWN_BATCH + 1) + 1)
            load_layer0(DOWN, e_next)
            e_b = pick(0, 1)
            for m in (6, 7):
                sp.wait_ge(s_w_lo, piece(0, m - 6) + 1)
                load_piece(m, e_b)

            def store(b):
                sp.wait_ge(s_y, b + 2)
                for q in range(Q):
                    sp.dma_start(out_blocks[bass.ds(b, 1), q].rearrange("o r n k -> (o r) n k"),
                                 y[q * BLK:(q + 1) * BLK, :, :]).then_inc(s_out, 16)

            def rest_of_b(b):
                e = pick(b, 1)
                for m in range(8, PIECES):
                    sp.wait_ge(s_w_lo, piece(b, m - 6) + 1)
                    load_piece(m, e)

            def sample(b, layer0):
                rest_of_b(b)
                if layer0:
                    e0 = pick(b + 2, 0)
                    sp.wait_ge(s_tr, batch(b + 1, X_BATCH) + 1)
                    load_x(b + 2)
                    sp.wait_ge(s_tr, batch(b + 1, UP_BATCH + 1) + 1)
                    load_layer0(UP, e0)
                    sp.wait_ge(s_tr, batch(b + 1, GATE_BATCH + 1) + 1)
                    load_layer0(GATE, e0)
                    sp.wait_ge(s_tr, batch(b + 1, DOWN_BATCH + 1) + 1)
                    load_layer0(DOWN, e0)
                e_first = pick(b + 1, 0)
                for m in range(6):
                    sp.wait_ge(s_w_lo, piece(b, m + 6) + 1)
                    load_piece(m, e_first)
                e_second = pick(b + 1, 1)
                sp.wait_ge(s_w_lo, piece(b + 1, 0) + 1)
                load_piece(6, e_second)
                store(b)
                sp.wait_ge(s_w_lo, piece(b + 1, AHEAD) + 1)
                load_piece(7, e_second)

            with loop(sp, B - 2) as b:
                sample(b, True)
            sample(B - 2, False)
            rest_of_b(B - 1)
            store(B - 1)
            sp.wait_ge(s_out, 16 * (Q * B + 1))

        @block.gpsimd
        def _(pool):
            def load_bias(k, bias, loaded):
                for q in range(Q):
                    pool.dma_start(bias_rows[:, k, q * BLK:(q + 1) * BLK],
                                   bias.rearrange("e (q c r) -> q e c r", q=Q, c=HC)[q]).then_inc(loaded, 16)

            pool.sem_inc(s_out, 16)
            pool.sem_inc(s_y, 1)
            nc.gpsimd.memset(ident[:, :], 0.0).then_inc(s_ident0, 1)
            nc.gpsimd.memset(ones[:, :], 1.0).then_inc(s_ident, 1)
            pool.wait_ge(s_ident0, 1)
            nc.gpsimd.affine_select(out=ident[:, :], in_=ident[:, :], compare_op=ALU.not_equal, fill=1.0,
                                    base=0, pattern=[[-1, P]], channel_multiplier=1).then_inc(s_ident, 1)
            load_bias(0, up0_b, s_bias_up)
            load_bias(1, gate0_b, s_bias)
            pool.dma_start(bias_down_rows[:, :], down0_b[:, :]).then_inc(s_bias, 16)
            for m in range(SHARED_PIECES):
                half, kind = m // 3, m % 3
                pool.wait_ge(s_shared_hi, m + 1)
                nc.gpsimd.tensor_tensor(split_view(w_lo[2 + half][kind], kind), raw_order(raw[half][kind], kind),
                                        split_view(w_hi[2 + half][kind], kind).bitcast(F32),
                                        ALU.subtract).then_inc(s_shared_lo, 1)

        @block.scalar
        def _(act):
            def split_hi(m, place, nth, done):
                h, kind = m // 3 % 2, m % 3
                act.wait_ge(s_raw[h][kind], 16 * nth)
                nc.scalar.activation(split_view(w_hi[place][kind], kind), raw_order(raw[h][kind], kind),
                                     ACT.Copy).then_inc(done, 1)

            def split_hi_shared(m):
                split_hi(m, 2 + m // 3, 1, s_shared_hi)

            def split_hi_routed(b, m):
                if m >= PIECES:
                    b, m = b + 1, m - PIECES
                split_hi(m, m // 3 % 2, 2 * b + m // 6 + 2, s_w_hi)

            def transposed_hi(s, i):
                act.wait_ge(s_tr, batch(s, i) + 1)
                turned_cols, hi, _ = batch_views(i)
                nc.scalar.activation(hi, turned_cols, ACT.Copy).then_inc(s_tr_hi, 1)

            def activate(n, r, kind, k, e, first=False):
                if first:
                    act.wait_ge(s_up0, n + 1)
                else:
                    act.wait_ge(s_gu, n + 1)
                if kind == "L":
                    for c in range(2):
                        ins = nc.scalar.activation(act_out[:, r, c, :], up_ps[r][:, c, :], ACT.Silu,
                                                   bias=bias_up[:, bass.ds(e * HC + 2 * k + c, 1)])
                    ins.then_inc(s_act, 1)
                else:
                    nc.scalar.activation(act_out[:, r, :, :].rearrange("p a b -> p (a b)"),
                                         gate_ps[r][:, :, :].rearrange("p a b -> p (a b)"),
                                         ACT.Gelu_apprx_tanh).then_inc(s_act, 1)

            def hidden_hi(n, r, used=True):
                act.wait_ge(s_mul, n + 1)
                if used:
                    act.wait_ge(s_down, n - 1)
                nc.scalar.activation(h_hi[r][:, :, :].rearrange("p a b -> p (a b)"),
                                     hidden[:, r, :, :].rearrange("p a b -> p (a b)"), ACT.Copy).then_inc(s_h_hi, 1)

            def last_activate(n, r):
                act.wait_ge(s_gu, n + 1)
                for c, done in enumerate((s_act_c0, s_act)):
                    nc.scalar.activation(act_out[:, r, c, :], gate_ps[r][:, c, :],
                                         ACT.Gelu_apprx_tanh).then_inc(done, 1)

            def last_hidden_hi(n, r, b):
                act.wait_ge(s_down, n - 1)
                act.wait_ge(s_mul_c0, b + 1)
                nc.scalar.activation(h_hi[r][:, 0, :], hidden[:, r, 0, :], ACT.Copy).then_inc(s_h_hi_c0, 1)
                act.wait_ge(s_mul, n + 1)
                nc.scalar.activation(h_hi[r][:, 1, :], hidden[:, r, 1, :], ACT.Copy).then_inc(s_h_hi, 1)

            def next_x1_hi(s):
                act.wait_ge(s_x1T, s + 1)
                nc.scalar.activation(x1_hi[:, :, :].rearrange("p a b -> p (a b)"),
                                     x1T[:, :, :].rearrange("p a b -> p (a b)"), ACT.Copy).then_inc(s_x1_hi, 1)

            def keep_residual(b):
                act.wait_ge(s_y, b + 1)
                nc.scalar.activation(total[:, :, :].rearrange("p a b -> p (a b)"),
                                     x1T[:, :, :].rearrange("p a b -> p (a b)"), ACT.Copy).then_inc(s_res, 1)

            def pick(s):
                return act.value_load(expert[0:1, bass.ds(s, 1), 0:1].rearrange("p a b -> p (a b)"),
                                      min_val=0, max_val=E - 1)

            act.wait_ge(s_top, 1)
            nc.scalar.activation(exps[:, :], top[:, :], ACT.Exp, bias=neg_max[:, 0:1],
                                 accum_out=exp_sum[:, 0:1]).then_inc(s_exp, 1)

            nc.scalar.preload_act_table(ACT.Silu)
            transposed_hi(0, X_BATCH)
            act.wait_ge(s_expert, 1)
            e0 = pick(0)
            for i in range(UP_BATCH, DOWN_BATCH):
                transposed_hi(0, i)
            act.wait_ge(s_bias_up_cols, 1)
            for k in range(2):
                activate(k, k, "L", k, e0, first=True)
            for i in range(DOWN_BATCH, BATCHES):
                transposed_hi(0, i)
            split_hi_shared(0)
            for k in range(2):
                hidden_hi(k, k, used=False)
            for m in (1, 2):
                split_hi_shared(m)
            nc.scalar.preload_act_table(ACT.Gelu_apprx_tanh)
            split_hi_shared(3)
            next_x1_hi(0)
            for m in range(4, SHARED_PIECES):
                split_hi_shared(m)
            split_hi_routed(0, 0)

            with loop(act, B - 1) as b:
                e0 = pick(b + 1)
                split_hi_routed(b, AHEAD)
                for j, (kind, k) in enumerate(PLAN[:-1]):
                    n = position(b, j)
                    activate(n, j % 2, kind, k, e0)
                    hidden_hi(n, j % 2)
                    if j in BATCH_AT:
                        transposed_hi(b + 1, BATCH_AT[j])
                    if j == KEEP_AT:
                        keep_residual(b)
                    for m in SPLIT_AT.get(j, ()):
                        split_hi_routed(b, m)
                n, r = position(b, NPOS - 1), (NPOS - 1) % 2
                last_activate(n, r)
                next_x1_hi(b + 1)
                last_hidden_hi(n, r, b)
            b = B - 1
            split_hi_routed(b, AHEAD)
            for j, (kind, k) in enumerate(LAST_PLAN[:-1]):
                n = position(b, j)
                activate(n, j % 2, kind, k, None)
                hidden_hi(n, j % 2)
                if j == KEEP_AT:
                    keep_residual(b)
                for m in LAST_SPLIT_AT.get(j, ()):
                    split_hi_routed(b, m)
            n, r = position(b, len(LAST_PLAN) - 1), (len(LAST_PLAN) - 1) % 2
            last_activate(n, r)
            last_hidden_hi(n, r, b)

        @block.vector
        def _(dve):
            def split_lo_routed(b, m):
                if m >= PIECES:
                    b, m = b + 1, m - PIECES
                h, kind = m // 3 % 2, m % 3
                dve.wait_ge(s_w_hi, piece(b, m) + 1)
                nc.vector.tensor_tensor(split_view(w_lo[h][kind], kind), raw_order(raw[h][kind], kind),
                                        split_view(w_hi[h][kind], kind).bitcast(F32),
                                        ALU.subtract).then_inc(s_w_lo, 1)

            def transpose_batch(s, i):
                if i >= 3:
                    dve.wait_ge(s_tr_lo, batch(s, i - 2) + 1)
                if i == X_BATCH:
                    dve.wait_ge(s_x, 16 * Q * (s + 1))
                    dst = xT[:, :, :].rearrange("p c (n r) -> p c n r", r=BLK)
                    src = x_raw[:, :, :].rearrange("p n (a c) -> p c n a", c=DC)
                elif i < DOWN_BATCH:
                    kind, dc = (UP, i - UP_BATCH) if i < GATE_BATCH else (GATE, i - GATE_BATCH)
                    dve.wait_ge(s_w0[kind], 16 * Q * (s + 1))
                    raw0 = up0_raw if kind == UP else gate0_raw
                    dst = turned[i % 2][:, :].rearrange("p (c q r) -> p q c r", c=HC, q=Q)
                    src = raw0[:, :, :].rearrange("p (q c) (a k) -> p k q c a", q=Q, k=DC)[:, dc]
                else:
                    dve.wait_ge(s_w0[DOWN], 16 * Q * (s + 1))
                    k = 2 * (i - DOWN_BATCH)
                    dst = turned[i % 2][:, :].rearrange("p (c n r) -> p c n r", c=2, r=BLK)
                    src = down0_raw[:, :, k * BLK:(k + 2) * BLK].rearrange("p n (c a) -> p c n a", c=2)
                nc.vector.transpose(dst, src).then_inc(s_tr, 1)

            def transposed_lo(s, i):
                dve.wait_ge(s_tr_hi, batch(s, i) + 1)
                turned_cols, hi, lo = batch_views(i)
                nc.vector.tensor_tensor(lo, turned_cols, hi.bitcast(F32), ALU.subtract).then_inc(s_tr_lo, 1)

            def multiply(n, r, kind, k, b, e, first=False):
                dve.wait_ge(s_act, n + 1)
                if first:
                    dve.wait_ge(s_gu, n + 1)
                flat = "p a b -> p (a b)"
                if kind == "L":
                    for c in range(2):
                        ins = nc.vector.scalar_tensor_tensor(
                            out=hidden[:, r, c, :], in0=gate_ps[r][:, c, :],
                            scalar=bias_gate[:, bass.ds(e * HC + 2 * k + c, 1)], in1=act_out[:, r, c, :],
                            op0=ALU.add, op1=ALU.mult)
                    ins.then_inc(s_mul, 1)
                elif kind == "S":
                    nc.vector.tensor_tensor(hidden[:, r, :, :].rearrange(flat), up_ps[r][:, :, :].rearrange(flat),
                                            act_out[:, r, :, :].rearrange(flat), ALU.mult).then_inc(s_mul, 1)
                else:
                    nc.vector.scalar_tensor_tensor(
                        out=hidden[:, r, :, :].rearrange(flat), in0=act_out[:, r, :, :].rearrange(flat),
                        scalar=route[:, bass.ds(b, 1), "AB".index(kind):"AB".index(kind) + 1].rearrange(flat),
                        in1=up_ps[r][:, :, :].rearrange(flat), op0=ALU.mult, op1=ALU.mult).then_inc(s_mul, 1)

            def hidden_lo(n, r):
                dve.wait_ge(s_h_hi, n + 1)
                flat = "p a b -> p (a b)"
                nc.vector.tensor_tensor(h_lo[r][:, :, :].rearrange(flat), hidden[:, r, :, :].rearrange(flat),
                                        h_hi[r][:, :, :].rearrange(flat).bitcast(F32), ALU.subtract).then_inc(s_h_lo, 1)

            def last_multiply(n, r, b):
                for c, (ready, value, done) in enumerate(((s_act_c0, b + 1, s_mul_c0), (s_act, n + 1, s_mul))):
                    dve.wait_ge(ready, value)
                    nc.vector.scalar_tensor_tensor(
                        out=hidden[:, r, c, :], in0=act_out[:, r, c, :],
                        scalar=route[:, bass.ds(b, 1), 1:2].rearrange("p a b -> p (a b)"),
                        in1=up_ps[r][:, c, :], op0=ALU.mult, op1=ALU.mult).then_inc(done, 1)

            def last_hidden_lo(n, r, b):
                for c, (ready, value, done) in enumerate(((s_h_hi_c0, b + 1, s_h_lo_c0), (s_h_hi, n + 1, s_h_lo))):
                    dve.wait_ge(ready, value)
                    nc.vector.tensor_tensor(h_lo[r][:, c, :], hidden[:, r, c, :], h_hi[r][:, c, :].bitcast(F32),
                                            ALU.subtract).then_inc(done, 1)

            def next_x1T(s, n, e, first=False):
                if not first:
                    dve.wait_ge(s_res, s)
                dve.wait_ge(s_down, n + 1)
                for dc in range(DC):
                    ins = nc.vector.scalar_tensor_tensor(
                        out=x1T[:, dc, :], in0=sum0_ps[dc][:, 0:S],
                        scalar=bias_down[:, bass.ds(e + dc * E, 1)],
                        in1=xT[:, dc, :], op0=ALU.add, op1=ALU.add)
                ins.then_inc(s_x1T, 1)

            def next_x1_lo(s):
                dve.wait_ge(s_x1_hi, s + 1)
                flat = "p a b -> p (a b)"
                nc.vector.tensor_tensor(x1_lo[:, :, :].rearrange(flat), x1T[:, :, :].rearrange(flat),
                                        x1_hi[:, :, :].rearrange(flat).bitcast(F32), ALU.subtract).then_inc(s_x1_lo, 1)

            def finish(b, n_last):
                dve.wait_ge(s_down, n_last + 1)
                dve.wait_ge(s_res, b + 1)
                for dc in range(DC):
                    ins = nc.vector.tensor_tensor(total[:, dc, :], out_ps[dc][:, 0:S], total[:, dc, :], ALU.add)
                ins.then_inc(s_free, 1)
                dve.wait_ge(s_free, b + 2)
                dve.wait_ge(s_out, 16 * (Q * b + 1))
                nc.vector.transpose(y[:, :, :].rearrange("p n (a c) -> p c n a", c=DC),
                                    total[:, :, :].rearrange("p c (n r) -> p c n r", r=BLK)).then_inc(s_y, 1)

            def pick(s):
                return dve.value_load(expert[0:1, bass.ds(s, 1), 0:1].rearrange("p a b -> p (a b)"),
                                      min_val=0, max_val=E - 1)

            links = [0]

            def chained(ins):
                links[0] += 1
                ins.then_inc(s_chain, 1)
                dve.wait_ge(s_chain, links[0])

            dve.wait_ge(s_cond, 16)
            chained(nc.vector.max(top[:, :], logits[:, :]))
            nc.vector.tensor_scalar(neg_max[:, :], top[:, 0:1], -1.0, None, ALU.mult).then_inc(s_top, 1)
            nc.vector.max_index(top_at[:, :], top[:, :], logits[:, :]).then_inc(s_top_at, 1)
            dve.wait_ge(s_top_at, 1)
            chained(nc.vector.tensor_copy(choice[:, :], top_at[:, 0:2]))

            def diagonal(dst, src):
                return nc.vector.tensor_tensor(dst[:, :, :],
                                               src[:, :].rearrange("p (o c) -> p o c", o=1).to_broadcast([B, B, 2]),
                                               ident[0:B, 0:B].rearrange("p (b o) -> p b o", o=1).to_broadcast([B, B, 2]),
                                               ALU.mult)

            dve.wait_ge(s_ident, 2)
            diagonal(choice_diag, choice).then_inc(s_diag, 1)
            dve.wait_ge(s_exp, 1)
            chained(nc.vector.reciprocal(exp_inv[:, :], exp_sum[:, :]))
            dve.wait_ge(s_spread, 1)
            nc.vector.tensor_copy(expert[:, :, :].rearrange("p b c -> p (b c)"), sum0_ps[1][:, 0:2 * B]).then_inc(s_expert, 1)
            chained(nc.vector.tensor_scalar(probs[:, :], exps[:, 0:2], exp_inv[:, 0:1], None, ALU.mult))
            chained(nc.vector.tensor_tensor(pair_sum[:, :], probs[:, 0:1], probs[:, 1:2], ALU.add))
            chained(nc.vector.reciprocal(pair_inv[:, :], pair_sum[:, :]))
            chained(nc.vector.tensor_scalar(pair_w[:, :], probs[:, :], pair_inv[:, 0:1], None, ALU.mult))
            chained(nc.vector.tensor_scalar(pair_w2[:, :], pair_w[:, :], 1.0 - MIX, None, ALU.mult))
            chained(nc.vector.scalar_tensor_tensor(out=weight[:, :], in0=pair_w[:, :], scalar=MIX, in1=pair_w2[:, :],
                                                   op0=ALU.mult, op1=ALU.add))
            diagonal(weight_diag, weight).then_inc(s_wdiag, 1)

            transpose_batch(0, X_BATCH)
            transposed_lo(0, X_BATCH)
            dve.wait_ge(s_wspread, 1)
            nc.vector.tensor_copy(route[:, :, :].rearrange("p b c -> p (b c)"), out_ps[0][:, 0:2 * B]).then_inc(s_route, 1)
            dve.wait_ge(s_expert, 1)
            e0 = pick(0)
            for i in (UP_BATCH, UP_BATCH + 1):
                transpose_batch(0, i)
            for i in (UP_BATCH, UP_BATCH + 1):
                transposed_lo(0, i)
            dve.wait_ge(s_biasT, 1)
            nc.vector.tensor_copy(bias_up[:, :], out_ps[1][:, 0:E * HC]).then_inc(s_bias_up_cols, 1)
            for i in (GATE_BATCH, GATE_BATCH + 1):
                transpose_batch(0, i)
            for i in (GATE_BATCH, GATE_BATCH + 1):
                transposed_lo(0, i)
            for i in (DOWN_BATCH, DOWN_BATCH + 1):
                transpose_batch(0, i)
            dve.wait_ge(s_biasT, 2)
            nc.vector.tensor_copy(bias_gate[:, :], out_ps[1][:, P:P + E * HC])
            nc.vector.tensor_copy(bias_down[:, :], out_ps[1][:, 2 * P:2 * P + E * DC]).then_inc(s_free, 1)
            dve.wait_ge(s_free, 1)
            transposed_lo(0, DOWN_BATCH)
            for k in range(2):
                multiply(k, k, "L", k, None, e0, first=True)
            hidden_lo(0, 0)
            transposed_lo(0, DOWN_BATCH + 1)
            hidden_lo(1, 1)
            next_x1T(0, 1, e0, first=True)
            next_x1_lo(0)
            dve.wait_ge(s_route, 1)
            split_lo_routed(0, 0)

            x1_at = PLAN.index(("L", 1)) + LAG + 1
            with loop(dve, B - 1) as b:
                e0 = pick(b + 1)
                split_lo_routed(b, AHEAD)
                for j, (kind, k) in enumerate(PLAN[:-1]):
                    n = position(b, j)
                    if j == x1_at:
                        next_x1T(b + 1, position(b, j - LAG - 1), e0)
                    multiply(n, j % 2, kind, k, b, e0)
                    if j in BATCH_AT:
                        transpose_batch(b + 1, BATCH_AT[j])
                    for m in SPLIT_AT.get(j - 1, ()):
                        split_lo_routed(b, m)
                    hidden_lo(n, j % 2)
                    if j in BATCH_AT:
                        transposed_lo(b + 1, BATCH_AT[j])
                n, r = position(b, NPOS - 1), (NPOS - 1) % 2
                last_multiply(n, r, b)
                last_hidden_lo(n, r, b)
                next_x1_lo(b + 1)
                finish(b, n)
            b = B - 1
            split_lo_routed(b, AHEAD)
            for j, (kind, k) in enumerate(LAST_PLAN[:-1]):
                n = position(b, j)
                multiply(n, j % 2, kind, k, b, None)
                for m in LAST_SPLIT_AT.get(j - 1, ()):
                    split_lo_routed(b, m)
                hidden_lo(n, j % 2)
            n, r = position(b, len(LAST_PLAN) - 1), (len(LAST_PLAN) - 1) % 2
            last_multiply(n, r, b)
            last_hidden_lo(n, r, b)
            finish(b, n)

        @block.tensor
        def _(pe):
            def three_passes(ps, w, m, first, last):
                nc.tensor.matmul(ps, w[0], m[0], start=first, stop=False)
                nc.tensor.matmul(ps, w[0], m[1], start=False, stop=False)
                return nc.tensor.matmul(ps, w[1], m[0], start=False, stop=last)

            def gate_up(n, r, kind, k):
                pe.wait_ge(s_mul, n - 1)
                for c in range(2):
                    for ps, what in ((gate_ps, GATE), (up_ps, UP)):
                        for dc in range(DC):
                            if kind == "L":
                                col = slice((2 * k + c) * P, (2 * k + c + 1) * P)
                                hi, lo = (gate0_hi, gate0_lo) if what == GATE else (up0_hi, up0_lo)
                                w = hi[:, dc, col], lo[:, dc, col]
                                m = xT_hi[:, dc, :], xT_lo[:, dc, :]
                            else:
                                w = chunk(half_of(kind, k), what, dc, 2 * (k % 2) + c)
                                m = x1_hi[:, dc, :], x1_lo[:, dc, :]
                            ins = three_passes(ps[r][:, c, :], w, m, dc == 0, dc == DC - 1)
                ins.then_inc(s_gu, 1)

            def down(n, r, kind, k, first, last, b=None):
                if not last:
                    pe.wait_ge(s_h_lo, n + 1)
                if kind == "L":
                    for c in range(2):
                        hc = 2 * k + c
                        for dc in range(DC):
                            col = slice(dc * P, (dc + 1) * P)
                            ins = three_passes(sum0_ps[dc][:, 0:S],
                                               (down0_hi[:, hc, col], down0_lo[:, hc, col]),
                                               (h_hi[r][:, c, :], h_lo[r][:, c, :]),
                                               hc == 0, hc == HC - 1)
                else:
                    place = half_of(kind, k)
                    for c in range(2):
                        if last:
                            pe.wait_ge(*((s_h_lo_c0, b + 1) if c == 0 else (s_h_lo, n + 1)))
                        for dc in range(DC):
                            at = (2 * (k % 2) + c) * D + dc * P
                            ins = three_passes(out_ps[dc][:, 0:S],
                                               (w_hi[place][DOWN][:, at:at + P], w_lo[place][DOWN][:, at:at + P]),
                                               (h_hi[r][:, c, :], h_lo[r][:, c, :]),
                                               first and c == 0, last and c == 1)
                ins.then_inc(s_down, 1)

            def bias_to_columns(k):
                return nc.tensor.transpose(out_ps[1][:, k * P:k * P + E * HC], bias_rows[:, k, :],
                                           ident[0:E * HC, 0:E * HC])

            pe.wait_ge(s_ident, 2)
            pe.wait_ge(s_diag, 1)
            nc.tensor.matmul(sum0_ps[1][:, 0:2 * B], ones[:, :], choice_diag[:, :, :].rearrange("p a b -> p (a b)"),
                             start=True, stop=True).then_inc(s_spread, 1)
            pe.wait_ge(s_wdiag, 1)
            nc.tensor.matmul(out_ps[0][:, 0:2 * B], ones[:, :], weight_diag[:, :, :].rearrange("p a b -> p (a b)"),
                             start=True, stop=True).then_inc(s_wspread, 1)

            def keep_warm(ps, count):
                for _ in range(count):
                    nc.tensor.matmul(ps[:, 0:P], ident[:, :], ident[:, :], start=True, stop=True)

            keep_warm(sum0_ps[0], WARM_LOADS)
            pe.wait_ge(s_bias_up, 16 * Q)
            bias_to_columns(0).then_inc(s_biasT, 1)
            for ps, hi, lo, first, done in ((up_ps, up0_hi, up0_lo, UP_BATCH, s_up0),
                                            (gate_ps, gate0_hi, gate0_lo, GATE_BATCH, s_gu)):
                for dc in range(DC):
                    pe.wait_ge(s_tr_lo, batch(0, first + dc) + 1)
                    for r in range(2):
                        for c in range(2):
                            col = slice((2 * r + c) * P, (2 * r + c + 1) * P)
                            for a, (w, m) in enumerate(((hi, xT_hi), (hi, xT_lo), (lo, xT_hi))):
                                ins = nc.tensor.matmul(ps[r][:, c, :], w[:, dc, col], m[:, dc, :],
                                                       start=(dc == 0 and c == 0 and a == 0),
                                                       stop=(dc == DC - 1 and a == 2), skip_group_check=True)
                        if dc == DC - 1:
                            ins.then_inc(done, 1)
                if ps is up_ps:
                    pe.wait_ge(s_bias, 16 * (Q + 1))
                    pe.wait_ge(s_bias_up_cols, 1)
                    bias_to_columns(1)
                    for dc in range(DC):
                        at = 2 * P + dc * E
                        ins = nc.tensor.transpose(out_ps[1][:, at:at + E],
                                                  bias_down_rows[:, :].rearrange("e (p c) -> e c p", c=DC)[:, dc, :],
                                                  ident[0:E, 0:E])
                    ins.then_inc(s_biasT, 1)
            keep_warm(sum0_ps[0], WARM_HIDDEN)
            pe.wait_ge(s_expert, 1)
            for k in range(2):
                pe.wait_ge(s_tr_lo, batch(0, DOWN_BATCH + k) + 1)
                down(k, k, "L", k, False, False)
            pe.wait_ge(s_route, 1)
            keep_warm(out_ps[0], WARM_X1)
            pe.wait_ge(s_shared_lo, 2)

            def sample(b, plan, layer0):
                steps = len(plan)
                pe.wait_ge(s_x1_lo, b + 1)
                for j in range(steps + LAG):
                    if j < steps:
                        kind, k = plan[j]
                        if kind in "AB" and k % 2 == 0:
                            pe.wait_ge(s_w_lo, piece(b, 6 * (kind == "B") + 3 * (k // 2) + UP) + 1)
                        if (kind, k) == ("S", 2):
                            pe.wait_ge(s_shared_lo, 5)
                        if kind == "L" and k == 0:
                            pe.wait_ge(s_tr_lo, batch(b + 1, GATE_BATCH + 1) + 1)
                        gate_up(position(b, j), j % 2, kind, k)
                    if j >= LAG:
                        kind, k = plan[j - LAG]
                        if kind in "AB" and k % 2 == 0:
                            pe.wait_ge(s_w_lo, piece(b, 6 * (kind == "B") + 3 * (k // 2) + DOWN) + 1)
                        if kind == "S" and k % 2 == 0:
                            pe.wait_ge(s_shared_lo, 3 * (k // 2) + DOWN + 1)
                        if kind == "L" and k == 0:
                            pe.wait_ge(s_tr_lo, batch(b + 1, DOWN_BATCH + 1) + 1)
                            pe.wait_ge(s_x1T, b + 1)
                        if j == LAG:
                            pe.wait_ge(s_free, b + 1)
                        down(position(b, j - LAG), j % 2, kind, k, j == LAG, j == steps + LAG - 1, b)

            with loop(pe, B - 1) as b:
                sample(b, PLAN, True)
            sample(B - 1, LAST_PLAN, False)


_INS = ['x', 'cond_8', 'L0_cond_W_up', 'L0_cond_b_up', 'L0_cond_W_gate', 'L0_cond_b_gate', 'L0_cond_W_down',
        'L0_cond_b_down', 'L1_cond_skill_gate', 'L1_cond_skill_up', 'L1_cond_skill_down', 'L1_cond_shared_gate',
        'L1_cond_shared_up', 'L1_cond_shared_down']


def kernel(**inputs):
    import numpy as _np
    import concourse.bacc as _bacc
    from concourse import mybir as _mybir
    from concourse.bass_utils import run_bass_kernel_spmd as _run

    nc = _bacc.Bacc("TRN2", target_bir_lowering=False, num_devices=1)
    arrays, args = {}, []
    for name in _INS:
        a = _np.ascontiguousarray(inputs[name])
        arrays[f"in_{name}_dram"] = a
        args.append(nc.dram_tensor(f"in_{name}_dram", a.shape, _mybir.dt.from_np(a.dtype), kind="ExternalInput").ap())
    shape = arrays["in_x_dram"].shape
    args.append(nc.dram_tensor("out_dram", shape, _mybir.dt.float32, kind="ExternalOutput").ap())
    bass_cond_two_layer_kernel(nc, *args)
    r = _run(nc, [arrays], core_ids=[0])
    return r.results[0]["out_dram"]
```
